# Optimizing a Trainium2 kernel written in Bass

```python
import numpy as np
import jax
import jax.numpy as jnp

def _softmax(x, axis=-1):
    return jax.nn.softmax(x, axis=axis)

def _gelu(x):
    return jax.nn.gelu(x, approximate=True)

def _silu(x):
    return jax.nn.silu(x)

def _sigmoid(x):
    return jax.nn.sigmoid(x)

def _layernorm(x, axis=-1, eps=1e-05):
    m = jnp.mean(x, axis=axis, keepdims=True)
    v = jnp.var(x, axis=axis, keepdims=True)
    return (x - m) / jnp.sqrt(v + eps)

def _scatter_add(tgt, idx, src, axis=0):
    return tgt.at[idx].add(src)

def _segment_sum(src, seg, n):
    return jax.ops.segment_sum(src, seg, n)
kernel_name = 'mk_adj_resnorm_d4_adj_r2_9e31ba'

def setup_inputs(seed: int=0):
    np.random.seed(seed)
    _w = jnp.asarray

    def _rec_inputs():
        import jax
        import jax.numpy as jnp
        _gk = jax.random.key(seed)
        x = -0.000929 + 1 * jax.random.normal(jax.random.fold_in(_gk, 1), (4096, 64), jnp.float32)
        _a = jax.random.bernoulli(jax.random.fold_in(_gk, 2), 0.00390625, (4096, 4096))
        _a = jnp.logical_or(_a, jnp.swapaxes(_a, -1, -2))
        _a = jnp.logical_or(_a, jnp.eye(4096, dtype=bool))
        _af = _a.astype(jnp.float32)
        adj = _af
        return (x, adj)
    x, adj = _rec_inputs()

    def _L0_gnn_setup():
        import jax, jax.numpy as jnp
        import numpy as np
        N = 8192
        F_IN = 64
        F_OUT = 64
        key = jax.random.key(seed)
        k1, k2, k3 = jax.random.split(key, 3)
        x = jax.random.normal(k1, (N, F_IN), dtype=jnp.float32)
        adj = jax.random.randint(k2, (N, N), 0, 2).astype(jnp.float32)
        W = jax.random.normal(k3, (F_IN, F_OUT), dtype=jnp.float32) * (1.0 / np.sqrt(F_IN))
        b = jnp.zeros((F_OUT,), dtype=jnp.float32)
        return {'x': x, 'adj': adj, 'W': W, 'b': b}
    _L0_gnn_all = _L0_gnn_setup()
    _L0_gnn_in = {k: v for k, v in _L0_gnn_all.items() if k in ('W', 'b')}
    del _L0_gnn_all

    def _L1_gnn_setup():
        import jax, jax.numpy as jnp
        import numpy as np
        N = 2048
        F = 64
        H = 8
        D = 8
        key = jax.random.key(seed)
        k1, k2, k3, k4, k5, k6 = jax.random.split(key, 6)
        X = jax.random.normal(k1, (N, F), dtype=jnp.float32)
        A = (jax.random.uniform(k2, (N, N)) < 0.01).astype(jnp.float32)
        A = jnp.maximum(A, jnp.eye(N, dtype=jnp.float32))
        lim_w = np.sqrt(6.0 / (F + H * D)).astype(np.float32)
        W = jax.random.uniform(k3, (F, H * D), minval=-lim_w, maxval=lim_w, dtype=jnp.float32)
        lim_a = np.sqrt(6.0 / (1 + H * D)).astype(np.float32)
        att_self = jax.random.uniform(k4, (H, D), minval=-lim_a, maxval=lim_a, dtype=jnp.float32)
        att_neigh = jax.random.uniform(k5, (H, D), minval=-lim_a, maxval=lim_a, dtype=jnp.float32)
        bias = jnp.zeros((H, D), dtype=jnp.float32)
        return {'X': X, 'A': A, 'W': W, 'att_self': att_self, 'att_neigh': att_neigh, 'bias': bias}
    _L1_gnn_all = _L1_gnn_setup()
    _L1_gnn_in = {k: v for k, v in _L1_gnn_all.items() if k in ('W', 'att_self', 'att_neigh', 'bias')}
    del _L1_gnn_all

    def _L2_gnn_setup():
        import jax, jax.numpy as jnp
        import numpy as np
        N = 4096
        F_IN = 64
        F_OUT = 64
        K = 4
        key = jax.random.key(seed)
        k1, k2, k3 = jax.random.split(key, 3)
        x = jax.random.normal(k1, (N, F_IN), dtype=jnp.float32)
        L = jax.random.normal(k2, (N, N), dtype=jnp.float32) * (1.0 / np.sqrt(N))
        weight = jax.random.normal(k3, (K, F_IN, F_OUT), dtype=jnp.float32) * (1.0 / np.sqrt(F_IN))
        return {'x': x, 'L': L, 'weight': weight}
    _L2_gnn_all = _L2_gnn_setup()
    _L2_gnn_in = {k: v for k, v in _L2_gnn_all.items() if k in ('weight',)}
    del _L2_gnn_all

    def _L3_gnn_setup():
        import jax, jax.numpy as jnp
        import numpy as np
        F_CONST = 1.0
        B_CONST = 0.1
        R_CONST = 0.01
        N, DIM = (4096, 64)
        key = jax.random.key(seed)
        k1, k2 = jax.random.split(key)
        x = jax.random.uniform(k1, (N, DIM), dtype=jnp.float32)
        A = jax.random.uniform(k2, (N, N), dtype=jnp.float32)
        return {'t': 0, 'x': x, 'A': A}
    _L3_gnn_all = _L3_gnn_setup()
    _L3_gnn_in = {k: v for k, v in _L3_gnn_all.items() if k in ()}
    del _L3_gnn_all
    return {'x': x, 'adj': adj, 'L0_gnn_W': _L0_gnn_in['W'], 'L0_gnn_b': _L0_gnn_in['b'], 'L1_gnn_W': _L1_gnn_in['W'], 'L1_gnn_att_self': _L1_gnn_in['att_self'], 'L1_gnn_att_neigh': _L1_gnn_in['att_neigh'], 'L1_gnn_bias': _L1_gnn_in['bias'], 'L2_gnn_weight': _L2_gnn_in['weight']}

def reference(x, adj, L0_gnn_W, L0_gnn_b, L1_gnn_W, L1_gnn_att_self, L1_gnn_att_neigh, L1_gnn_bias, L2_gnn_weight):
    import jax
    import jax.numpy as jnp

    def _L0_gnn_ref(x, adj, W, b):
        import jax, jax.numpy as jnp
        import numpy as np
        N = 8192
        F_IN = 64
        F_OUT = 64
        deg = adj.sum(axis=0) + 1.0
        dinv = jnp.where(deg > 0, jax.lax.rsqrt(deg), 0.0)
        xw = x @ W
        z = dinv[:, None] * xw
        out = dinv[:, None] * (adj.T @ z + z) + b
        return jax.nn.relu(out)

    def _L1_gnn_ref(X, A, W, att_self, att_neigh, bias):
        import jax, jax.numpy as jnp
        import numpy as np
        N = 2048
        F = 64
        H = 8
        D = 8
        feats = (X @ W).reshape(-1, H, D)
        a_self = jnp.einsum('nhd,hd->nh', feats, att_self)
        a_neigh = jnp.einsum('nhd,hd->nh', feats, att_neigh)
        scores = a_self.T[:, :, None] + a_neigh.T[:, None, :]
        scores = jax.nn.leaky_relu(scores, negative_slope=0.2)
        scores = scores + (-10000000000.0 * (1.0 - A))[None, :, :]
        attn = jax.nn.softmax(scores, axis=-1)
        out = jnp.einsum('hij,jhd->ihd', attn, feats)
        out = out + bias[None, :, :]
        out = out.reshape(-1, H * D)
        return jax.nn.relu(out)

    def _L2_gnn_ref(x, L, weight):
        import jax, jax.numpy as jnp
        import numpy as np
        N = 4096
        F_IN = 64
        F_OUT = 64
        K = 4
        terms = [x, L @ x]
        for _ in range(2, K):
            terms.append(2.0 * (L @ terms[-1]) - terms[-2])
        feature = jnp.stack(terms, axis=0)
        return jnp.einsum('kni,kio->no', feature, weight)

    def _L3_gnn_ref(t, x, A):
        import jax, jax.numpy as jnp
        import numpy as np
        F_CONST = 1.0
        B_CONST = 0.1
        R_CONST = 0.01
        N, DIM = (4096, 64)
        Ax = A @ x
        outer = R_CONST * jnp.sum(x * Ax, axis=1, keepdims=True)
        return F_CONST - B_CONST * x - outer
    x = _layernorm(x + _L0_gnn_ref(x, adj, L0_gnn_W, L0_gnn_b), axis=-1)
    x = _layernorm(x + _L1_gnn_ref(x, adj, L1_gnn_W, L1_gnn_att_self, L1_gnn_att_neigh, L1_gnn_bias), axis=-1)
    x = _layernorm(x + _L2_gnn_ref(x, adj, L2_gnn_weight), axis=-1)
    x = _layernorm(x + _L3_gnn_ref(0, x, adj), axis=-1)
    return x

_drawn_inputs = setup_inputs


def setup_inputs(seed=0):
    import zlib

    import numpy as np

    out = dict(_drawn_inputs(seed))
    spreads = {'L0_gnn_b': (0.0, 0.1), 'L1_gnn_bias': (0.0, 0.1)}
    factors = {'L1_gnn_att_self': 9.302}
    for name, (base, spread) in spreads.items():
        noise = np.random.default_rng([zlib.crc32(name.encode()), seed]).standard_normal(out[name].shape)
        drawn = base * np.exp(spread * noise) if base else spread * noise
        out[name] = jnp.asarray(drawn.astype(out[name].dtype))
    for name, factor in factors.items():
        out[name] = (out[name] * factor).astype(out[name].dtype)
    return out
```

```python
from contextlib import ExitStack

import concourse.bass as bass
from concourse import mybir

P = 128
F32, BF16 = mybir.dt.float32, mybir.dt.bfloat16
FP8, U8, I32 = mybir.dt.float8e4, mybir.dt.uint8, mybir.dt.int32
ALU = mybir.AluOpType
ACT = mybir.ActivationFunctionType
AX_X = mybir.AxisListType.X
RMAX = bass.bass_isa.ReduceOp.max

ONE_FP8 = 56.0
STEP = float(2.0 ** 60)
SLOPE = 0.2
EPS = 1e-5
RING = 4
DVE_SHARE = 25, 64


def on_dve(k):
    part, whole = DVE_SHARE
    return (k + 1) * part // whole > k * part // whole


class Chain:

    def __init__(self, eng, sem, passed=None):
        self.passed = passed
        self.eng, self.sem, self.n, self.loop = eng, sem, 0, 0

    def __call__(self, ins):
        ins.then_inc(self.sem, 1)
        self.n += 1

    def wait(self):
        self.eng.wait_ge(self.sem, self.loop + self.n)
        if self.passed is not None:
            self.eng.sem_inc(self.passed, 1)

    def do(self, ins):
        self(ins)
        self.wait()

    def body(self, i, per):
        self.start, self.per, self.loop = self.n, per, i * per

    def end(self, count):
        assert self.n - self.start == self.per, (self.n - self.start, self.per)
        self.n, self.loop = self.start + self.per * count, 0


def graph_layers(nc, x, adj, w0, b0, w1, att_self, att_neigh, bias1, w2, out, sc_rows, sc_x):
    N, F = x.shape
    H, D = att_self.shape
    K = w2.shape[0]
    T = N // P
    TP = T // 2
    PAIRS = H // 2
    C = 2 * (D + 1)
    C3 = 3 * C
    PER_BANK = 512 // C3
    FN = F + 2 * H
    STEPS = 2 * T
    assert (N, F, H * D) == (4096, 64, F) and T % PER_BANK <= PER_BANK

    x_t = x.rearrange("(t p) f -> p t f", p=P)
    out_t = out.rearrange("(t p) f -> p t f", p=P)
    sc_x_t = sc_x.rearrange("(t p) f -> p t f", p=P)
    adj_t = adj.rearrange("(t p) n -> t p n", p=P)

    with ExitStack() as ctx:
        def sb(name, shape, dt=F32):
            return ctx.enter_context(nc.sbuf_tensor(name, shape, dt))

        def sem(name):
            return ctx.enter_context(nc.semaphore(name))

        adj8 = sb("adj8", [P, T, N], U8)
        big = sb("big", [P, 3 * N])
        feat = sb("feat", [P, T, F])
        aux = sb("aux", [P, 2 * T * C3], F32)
        r_h = sb("r_h", [P, 2, T, C])
        s_d = sb("s_d", [P, T, 2, D + 1])
        den = sb("den", [P, T, H])
        fac = sb("fac", [P, 4, T, H])
        n_cols = sb("n_cols", [P, 2, H, T])
        cols = sb("cols", [P, 2, 2 * T])
        n_cur, k_cur = cols[:, 0, :], cols[:, 1, :]
        g_val = sb("g_val", [P, T, 2, C])
        g_res = sb("g_res", [P, T, 2, C])
        ident = sb("ident", [P, P])
        b0_b = sb("b0_b", [P, F])
        b1_b = sb("b1_b", [P, F])
        deg = sb("deg", [P, T])
        dinv = sb("dinv", [P, T])
        root = sb("root", [P, T])
        stat = sb("stat", [P, T])
        nmax = sb("nmax", [P, 2, H])
        coef = sb("coef", [P, K])
        epsc = sb("epsc", [P, 1])

        bank = [ctx.enter_context(nc.psum_tensor(f"bank{b}", [P, 512], F32)) for b in range(8)]

        stage = [big[:, 0:N], big[:, N:2 * N]]
        row_buf = [big[:, 2 * N + N // 4 * r:2 * N + N // 4 * (r + 1)] for r in range(4)]
        zeros = row_buf[0].bitcast(BF16)[:, 0:512]
        x_tr = adj8[:, T - 4:T, :].rearrange("p a n -> p (a n)").bitcast(F32)[:, 0:TP * P]
        xw = aux[:, 0:T * F].rearrange("p (t f) -> p t f", f=F)
        z_res = aux[:, T * F:T * F + 2 * F].rearrange("p (a f) -> p a f", f=F)
        z_part = aux[:, T * F + 2 * F:T * F + 5 * F].bitcast(BF16).rearrange("p (u q f) -> p u q f", u=2, q=3)
        x1 = big[:, 0:T * F].rearrange("p (t f) -> p t f", f=F)
        work = big[:, N:N + T * F].rearrange("p (t f) -> p t f", f=F)
        x1_tr = big[:, 2 * N:2 * N + TP * P]
        s_rows = big[0:2 * H, N:N + TP * P]
        s_row = [big[:, 0:N], big[:, N:2 * N]]
        mask = [big[:, 2 * N + N // RING * r:2 * N + N // RING * (r + 1)] for r in range(RING)]
        g = aux[:, 0:T * C3].bitcast(BF16).rearrange("p (t e q c) -> p t e q c", t=T, e=2, q=3)
        g_next = aux[:, T * C3:2 * T * C3].bitcast(BF16).rearrange("p (t e q c) -> p t e q c", t=T, e=2, q=3)
        TF = T * F

        early = r_h[:, :, :, :].rearrange("p e t c -> p (e t c)")
        w0_d = early[:, 0:2 * F]
        w1_d = early[:, 2 * F:2 * F + 2 * FN].rearrange("p (e n) -> p e n", e=2)
        wsn = early[:, 4 * F + 2 * FN:4 * F + 2 * FN + 2 * H]
        w2_d = g_res[:, :, :, :].rearrange("p t e c -> p (t e c)")[:, 0:K * 2 * F].rearrange("p (k o) -> p k o", k=K)
        xt2 = g_val[:, :, :, :].rearrange("p t e c -> p (t e c)")[:, 0:2 * P].rearrange("p (a c) -> p a c", a=2)

        def term(k):
            return big[:, k * TF:(k + 1) * TF].rearrange("p (t f) -> p t f", f=F)
        t_cur, t_old, t_new = term(0), term(1), term(2)
        parts = big[:, 3 * TF:3 * TF + 3 * TF // 2].bitcast(BF16).rearrange("p (t q f) -> p t q f", q=3, f=F)
        parts_new = big[:, 3 * TF + 3 * TF // 2:6 * TF].bitcast(BF16).rearrange("p (t q f) -> p t q f", q=3, f=F)
        res2 = aux[:, 0:2 * F].rearrange("p (a f) -> p a f", f=F)
        big2 = aux[:, 0:T * F].rearrange("p (t f) -> p t f", f=F)

        x_loaded = sem("x_loaded")
        w_loaded = sem("w_loaded")
        w_zeroed = sem("w_zeroed")
        stage_loaded = [sem("stage0_loaded"), sem("stage1_loaded")]
        stage_read_act = sem("stage_read_act")
        stage_read_dve = sem("stage_read_dve")
        const_ready = sem("const_ready")
        dve_did = sem("dve_did")
        act_passed = sem("act_passed")
        pe_passed = sem("pe_passed")
        pool_passed = sem("pool_passed")
        act_did = sem("act_did")
        pool_did = sem("pool_did")
        tr_done = sem("tr_done")
        tr_copied = sem("tr_copied")
        prod_done = sem("prod_done")
        prod_copied = sem("prod_copied")
        zero_ready = sem("zero_ready")
        dinv_ready = sem("dinv_ready")
        root_ready = sem("root_ready")
        z_ready = sem("z_ready")
        rows_free = sem("rows_free")
        x1_ready = sem("x1_ready")
        var_ready = sem("var_ready")
        std_ready = sem("std_ready")
        w1_ready = sem("w1_ready")
        srow_done = sem("srow_done")
        srow_copied = sem("srow_copied")
        srow_stored = sem("srow_stored")
        x1_stored = sem("x1_stored")
        nmax_part = sem("nmax_part")
        nmax_ready = sem("nmax_ready")
        exp_in = sem("exp_in")
        exp_out = sem("exp_out")
        cols_ready = sem("cols_ready")
        row_loaded = [sem("row0_loaded"), sem("row1_loaded")]
        row_free = [sem("row0_free"), sem("row1_free")]
        cmp_act = sem("cmp_act")
        cmp_dve = sem("cmp_dve")
        mask_ready = sem("mask_ready")
        mask_free = sem("mask_free")
        acc_free = sem("acc_free")
        sd_done = sem("sd_done")
        sd_free = sem("sd_free")
        g_made = sem("g_made")
        g_loaded = sem("g_loaded")
        sums_ready = sem("sums_ready")
        sums_used = sem("sums_used")
        x1_back = sem("x1_back")
        w2_zeroed = sem("w2_zeroed")
        w2_loaded = sem("w2_loaded")
        terms_ready = sem("terms_ready")
        cur_ready = sem("cur_ready")
        shifted = sem("shifted")
        sp_done = sem("sp_done")
        sp_free = sem("sp_free")
        new_ready = sem("new_ready")
        xt_done = sem("xt_done")
        xt_copied = sem("xt_copied")
        y_added = sem("y_added")
        out_ready = sem("out_ready")
        out_stored = sem("out_stored")
        block = ctx.enter_context(nc.Block())

        HALF = T // 2
        L3G = 4

        def bcast(ap2, n):
            return ap2.unsqueeze(2).to_broadcast([P, ap2.shape[1], n])

        @block.sync
        def _(sp):
            sp.dma_start(feat[:, :, :], x_t).then_inc(x_loaded, 16)
            for u in range(2):
                sp.dma_start(stage[u], adj_t[u]).then_inc(stage_loaded[u], 16)
            with sp.Fori(1, HALF) as i:
                for u in range(2):
                    sp.wait_ge(stage_read_act, 2 * i + u - 1)
                    sp.wait_ge(stage_read_dve, 2 * i + u - 1)
                    sp.dma_start(stage[u], adj_t[bass.ds(2 * i + u, 1), :, :].rearrange("a p n -> (a p) n")).then_inc(stage_loaded[u], 16)
            sp.wait_ge(x1_ready, 1)
            sp.dma_start(sc_x_t, x1).then_inc(x1_stored, 16)
            sp.wait_ge(srow_copied, 4)
            sr = sc_rows.rearrange("h (k e c) -> e h k c", e=2, c=P)
            for e in range(2):
                sp.dma_start(sr[e], s_rows[e * H:(e + 1) * H, :].rearrange("p (k c) -> p k c", c=P)).then_inc(srow_stored, 16)
            sp.wait_ge(srow_stored, 32)
            sp.wait_ge(x1_stored, 16)
            sp.wait_ge(tr_done, 2 * TP)
            with sp.Fori(0, PAIRS) as pr:
                for e in range(2):
                    sp.wait_ge(row_free[e], 2 * pr + 2)
                    sp.dma_start(s_row[e], sc_rows[bass.ds(2 * pr + e, 1), :].to_broadcast([P, N])).then_inc(row_loaded[e], 16)
            sp.wait_ge(row_free[0], 2 * PAIRS + 2)
            sp.dma_start(x1, sc_x_t).then_inc(x1_back, 16)
            sp.wait_ge(w2_zeroed, 1)
            for e in range(2):
                sp.dma_start(w2_d[e * F:(e + 1) * F, :, e * F:(e + 1) * F], w2.rearrange("k i o -> i k o")).then_inc(w2_loaded, 16)
            for m in range(T // L3G):
                sp.wait_ge(out_ready, m + 1)
                sp.dma_start(out_t[:, L3G * m:L3G * (m + 1), :], feat[:, L3G * m:L3G * (m + 1), :]).then_inc(out_stored, 16)
            sp.wait_ge(out_stored, 16 * (T // L3G))

        @block.gpsimd
        def _(pool):
            chain = Chain(pool, pool_did, pool_passed)
            pool.sem_inc(row_free[0], 2)
            pool.sem_inc(row_free[1], 2)
            pool.sem_inc(sums_used, 1)
            chain.do(nc.gpsimd.memset(ident[:, :], 0.0))
            nc.gpsimd.affine_select(out=ident[:, :], in_=ident[:, :], compare_op=ALU.not_equal, fill=1.0,
                                    base=0, pattern=[[-1, P]], channel_multiplier=1).then_inc(const_ready, 1)
            pool.wait_ge(prod_copied, TP)
            with pool.Fori(0, HALF) as i:
                chain.body(i, 2 * 5)
                for u in range(2):
                    t = bass.ds(2 * i + u, 1)
                    pool.wait_ge(rows_free, 2 * i + u + 3)
                    pool.wait_ge(dinv_ready, 2 * i + u + 1)
                    pool.sem_inc(pool_passed, 1)
                    chain.do(nc.gpsimd.tensor_tensor(xw[:, t, :], xw[:, t, :], dinv[:, t].unsqueeze(2).to_broadcast([P, 1, F]), ALU.mult))
                    chain.do(nc.gpsimd.tensor_copy(z_part[:, u, 0:1, :], xw[:, t, :]))
                    chain.do(nc.gpsimd.tensor_tensor(z_res[:, 0:1, :], xw[:, t, :], z_part[:, u, 0:1, :], ALU.subtract))
                    chain.do(nc.gpsimd.tensor_copy(z_part[:, u, 1:2, :], z_res[:, 0:1, :]))
                    chain.do(nc.gpsimd.tensor_tensor(z_res[:, 1:2, :], z_res[:, 0:1, :], z_part[:, u, 1:2, :], ALU.subtract))
                    nc.gpsimd.tensor_copy(z_part[:, u, 2:3, :], z_res[:, 1:2, :]).then_inc(z_ready, 1)
                chain.end(HALF)
            pool.wait_ge(nmax_part, 1)
            nc.gpsimd.partition_all_reduce(nmax[:, 1, :], nmax[:, 0, :], P, RMAX).then_inc(nmax_ready, 1)

            def prepare(pr):
                fh = feat[:, :, bass.ds(pr * 2 * D, 2 * D)].rearrange("p t (e d) -> p t e d", e=2)
                for m, o in ((1, 0), (3, D + 1)):
                    fm = fac[:, m, :, bass.ds(pr * 2, 2)]
                    chain(nc.gpsimd.tensor_tensor(g_val[:, :, :, o:o + D], fh,
                                                  fm.unsqueeze(3).to_broadcast([P, T, 2, D]), ALU.mult))
                    chain(nc.gpsimd.tensor_copy(g_val[:, :, :, o + D], fm))
                chain.wait()
                chain.do(nc.gpsimd.tensor_copy(g_next[:, :, :, 0, :], g_val[:, :, :, :]))
                chain.do(nc.gpsimd.tensor_tensor(g_res[:, :, :, :], g_val[:, :, :, :], g_next[:, :, :, 0, :], ALU.subtract))
                chain.do(nc.gpsimd.tensor_copy(g_next[:, :, :, 1, :], g_res[:, :, :, :]))
                chain.do(nc.gpsimd.tensor_tensor(g_val[:, :, :, :], g_res[:, :, :, :], g_next[:, :, :, 1, :], ALU.subtract))
                nc.gpsimd.tensor_copy(g_next[:, :, :, 2, :], g_val[:, :, :, :]).then_inc(g_made, 1)

            def combine(pr, last):
                a = fac[:, 0, :, bass.ds(pr * 2, 2)]
                c = fac[:, 2, :, bass.ds(pr * 2, 2)]
                for e in range(2):
                    mb, md = r_h[:, e, :, 0:D + 1], r_h[:, e, :, D + 1:C]
                    chain(nc.gpsimd.tensor_tensor(md, s_d[:, :, e, :], md, ALU.subtract))
                    chain(nc.gpsimd.tensor_tensor(mb, mb, bcast(a[:, :, e], D + 1), ALU.mult))
                chain.wait()
                for e in range(2):
                    md = r_h[:, e, :, D + 1:C]
                    chain(nc.gpsimd.tensor_tensor(md, md, bcast(c[:, :, e], D + 1), ALU.mult))
                chain.wait()
                for e in range(2):
                    mb, md = r_h[:, e, :, 0:D + 1], r_h[:, e, :, D + 1:C]
                    chain(nc.gpsimd.tensor_tensor(feat[:, :, bass.ds((pr * 2 + e) * D, D)], mb[:, :, 0:D], md[:, :, 0:D], ALU.add))
                    ins = nc.gpsimd.tensor_tensor(den[:, :, bass.ds(pr * 2 + e, 1)], mb[:, :, D:D + 1], md[:, :, D:D + 1], ALU.add)
                    if e == 0:
                        chain(ins)
                chain.wait()
                ins.then_inc(sums_used, 1)

            pool.wait_ge(prod_copied, 2 * TP)
            pool.wait_ge(exp_out, 1)
            prepare(0)
            with pool.Fori(0, PAIRS - 1) as pr:
                chain.body(pr, 16 - 0 + 1)
                pool.wait_ge(g_loaded, pr + 1)
                prepare(pr + 1)
                pool.wait_ge(sums_ready, pr + 1)
                combine(pr, False)
                chain.end(PAIRS - 1)
            pool.wait_ge(sums_ready, PAIRS)
            combine(PAIRS - 1, True)

        @block.scalar
        def _(act):
            chain = Chain(act, act_did)
            act.wait_ge(w_zeroed, 1)
            nw = 0
            for e in range(2):
                rows = slice(e * F, (e + 1) * F)
                act.dma_start(w0_d[rows, e * F:(e + 1) * F], w0).then_inc(w_loaded, 16)
                act.dma_start(w1_d[rows, e, 0:F], w1).then_inc(w_loaded, 16)
            act.dma_start(b0_b[:, :], b0.rearrange("(a n) -> a n", a=1).to_broadcast([P, F])).then_inc(w_loaded, 16)
            act.dma_start(b1_b[:, :], bias1.rearrange("h d -> (h d)").rearrange("(a n) -> a n", a=1).to_broadcast([P, F])).then_inc(w_loaded, 16)
            for m, att in enumerate((att_self, att_neigh)):
                act.dma_start(g_val[:, 0:4, :, :].rearrange("p t e c -> p (t e c)")[:, m * F:(m + 1) * F],
                              att.rearrange("h d -> (h d)").rearrange("(a n) -> a n", a=1).to_broadcast([P, F])).then_inc(w_loaded, 16)

            def copy_transposed(dst, base):
                for k in range(TP):
                    act.wait_ge(tr_done, base + k + 1)
                    nc.scalar.activation(dst[:, k * P:(k + 1) * P], bank[4 + k % 2][:, 0:P], ACT.Copy).then_inc(tr_copied, 1)

            copy_transposed(x_tr, 0)
            act.wait_ge(prod_done, TP)
            def rows8(j, u, n):
                act.wait_ge(stage_loaded[u], 16 * n)
                nc.scalar.activation(adj8[:, bass.ds(j, 1), :].rearrange("p a n -> p (a n)"), stage[u], ACT.Copy, scale=ONE_FP8).then_inc(stage_read_act, 1)

            def degree_roots(j):
                act.wait_ge(stage_read_dve, j + 2)
                nc.scalar.activation(root[:, bass.ds(j, 2)], deg[:, bass.ds(j, 2)], ACT.Sqrt, bias=1.0, scale=1.0 / ONE_FP8).then_inc(root_ready, 2)

            rows8(0, 0, 1)
            with act.Fori(0, HALF - 1) as i:
                rows8(2 * i + 1, 1, i + 1)
                rows8(2 * i + 2, 0, i + 2)
                degree_roots(2 * i)
            rows8(T - 1, 1, HALF)
            degree_roots(T - 2)

            def norm_root(n, t0=0, t1=T):
                act.wait_ge(var_ready, n)
                nc.scalar.activation(root[:, t0:t1], stat[:, t0:t1], ACT.Sqrt, bias=epsc[:, 0:1], scale=1.0 / F).then_inc(std_ready, 1)

            norm_root(1)
            copy_transposed(x1_tr, TP)
            for b in range(4):
                act.wait_ge(srow_done, b + 1)
                nc.scalar.activation(s_rows[:, b * 512:(b + 1) * 512], bank[b][0:2 * H, :], ACT.Copy).then_inc(srow_copied, 1)
            act.wait_ge(exp_in, 1)
            nc.scalar.activation(fac[:, :, :, :], fac[:, :, :, :], ACT.Exp).then_inc(exp_out, 1)

            na = sum(not on_dve(k) for k in range(STEPS))
            with act.Fori(0, PAIRS) as pr:
                act.wait_ge(cols_ready, pr + 1)
                for e in range(2):
                    act.wait_ge(row_loaded[e], 16 * pr + 16)
                    mine = [k for k in range(e * T, (e + 1) * T) if not on_dve(k)]
                    for k in mine:
                        act.wait_ge(mask_free, STEPS * pr + k + 1)
                        act.sem_inc(act_passed, 1)
                        nc.scalar.activation(mask[k % RING].bitcast(FP8), s_row[e], ACT.Sigmoid,
                                             bias=k_cur[:, k:k + 1], scale=STEP, saturate=False).then_inc(cmp_act, 1)
                    act.wait_ge(cmp_act, na * pr + sum(not on_dve(k) for k in range((e + 1) * T)))
                    act.sem_inc(row_free[e], 1)
            norm_root(2)

            def copy_xt(n, k):
                act.wait_ge(xt_done, n + 1)
                nc.scalar.activation(xt2[:, k % 2, :], bank[6 + k % 2][:, 0:P], ACT.Copy).then_inc(xt_copied, 1)

            for k in range(TP):
                copy_xt(k, k)

            act.sem_inc(shifted, 1)
            with act.Fori(0, K - 2) as p:
                for k in range(TP):
                    copy_xt(TP * p + TP + k, k)
                act.wait_ge(new_ready, TP * p + TP)
                nc.scalar.activation(t_old, t_cur, ACT.Copy).then_inc(shifted, 1)
                act.wait_ge(shifted, 2 * p + 2)
                nc.scalar.activation(t_cur, t_new, ACT.Copy).then_inc(shifted, 1)
            for k in range(TP):
                copy_xt(TP * (K - 1) + k, k)
                if k % 4 == 0 and k >= 4:
                    norm_root(2 + k // 4, 2 * k - 8, 2 * k)
            norm_root(2 + TP // 4, T - 8, T)
            for m in range(T // L3G):
                norm_root(2 + TP // 4 + m + 1, L3G * m, L3G * (m + 1))

        @block.tensor
        def _(pe):
            pe.sem_inc(rows_free, 4)
            pe.sem_inc(mask_free, RING)
            pe.sem_inc(acc_free, 1)
            pe.sem_inc(sd_free, 2)
            pe.sem_inc(sp_free, 2)

            def weights_product(src, dst, w, ncol, base):
                for k in range(TP + 1):
                    if k < TP:
                        if k >= 2:
                            pe.wait_ge(tr_copied, base + k - 1)
                        nc.tensor.transpose(bank[4 + k % 2][:, 0:P], src[:, 2 * k:2 * k + 2, :].rearrange("p a f -> p (a f)"),
                                            ident[:, :]).then_inc(tr_done, 1)
                    if k >= 1:
                        j = k - 1
                        pe.wait_ge(tr_copied, base + j + 1)
                        if base + j >= 2:
                            pe.wait_ge(prod_copied, base + j - 1)
                        nc.tensor.matmul(bank[6 + j % 2][:, 0:ncol], dst[:, j * P:(j + 1) * P], w,
                                         start=True, stop=True).then_inc(prod_done, 1)

            pe.wait_ge(x_loaded, 16)
            pe.wait_ge(const_ready, 1)
            pe.wait_ge(w_loaded, 16 * 8)
            weights_product(feat, x_tr, w0_d[:, :], 2 * F, 0)

            pe.wait_ge(zero_ready, 1)
            for b in range(4):
                nc.tensor.matmul(bank[b][:, :], zeros[:, 0:P], zeros, start=True, stop=False, skip_group_check=True)\
                    .then_inc(prod_done, 1)
            with pe.Fori(0, T // 4) as i:
                for u in range(4):
                    pe.wait_ge(z_ready, 4 * i + u + 1)
                    pe.sem_inc(pe_passed, 1)
                    for it in range(T):
                        for q in range(3):
                            last = nc.tensor.matmul(bank[it // 8][:, (it % 8) * F:(it % 8 + 1) * F],
                                                    row_buf[u].bitcast(FP8)[:, it * P:(it + 1) * P], z_part[:, u % 2, q, :],
                                                    start=False, stop=False, skip_group_check=True)
                    last.then_inc(rows_free, 1)

            pe.wait_ge(x1_ready, 1)
            pe.wait_ge(w1_ready, 1)
            for k in range(TP + 1):
                if k < TP:
                    if k >= 2:
                        pe.wait_ge(tr_copied, TP + k - 1)
                    nc.tensor.transpose(bank[4 + k % 2][:, 0:P], x1[:, 2 * k:2 * k + 2, :].rearrange("p a f -> p (a f)"),
                                        ident[:, :]).then_inc(tr_done, 1)
                if k >= 1:
                    j = k - 1
                    pe.wait_ge(tr_copied, TP + j + 1)
                    if j >= 2:
                        pe.wait_ge(prod_copied, TP + j - 1)
                    nc.tensor.matmul(bank[6 + j % 2][:, 0:2 * FN], x1_tr[:, j * P:(j + 1) * P],
                                     w1_d[:, :, :].rearrange("p e n -> p (e n)"),
                                     start=True, stop=True).then_inc(prod_done, 1)
            for b in range(4):
                nc.tensor.matmul(bank[b][0:2 * H, :], wsn[:, 0:2 * H], x1_tr[:, b * 512:(b + 1) * 512],
                                 start=True, stop=True).then_inc(srow_done, 1)

            pe.wait_ge(srow_copied, 4)
            with pe.Fori(0, PAIRS) as pr:
                pe.wait_ge(g_loaded, pr + 1)
                for k in range(STEPS):
                    e, jt, t = k // T, k % T, k // 2
                    if jt == 0:
                        pe.wait_ge(acc_free, 2 * pr + e + 1)
                    pe.wait_ge(mask_ready, STEPS * pr + k + 1)
                    pe.sem_inc(pe_passed, 1)
                    m8 = mask[k % RING].bitcast(FP8)
                    for it in range(T):
                        c0 = it % PER_BANK * C3
                        last = nc.tensor.matmul(bank[it // PER_BANK][:, c0:c0 + C3], m8[:, it * P:(it + 1) * P],
                                                g[:, jt, e, :, :].rearrange("p q c -> p (q c)"),
                                                start=(jt == 0 and it % PER_BANK == 0), stop=(jt == T - 1), skip_group_check=True)
                    last.then_inc(mask_free, 1)
                    if k % 2 == 0:
                        pe.wait_ge(sd_free, T * pr + t + 1)
                        pe.sem_inc(pe_passed, 1)
                    for j in range(k % 2 * HALF, k % 2 * HALF + HALF):
                        last = nc.tensor.matmul(bank[4 + t % 2][:, 0:C3].rearrange("p (m c) -> p m c", c=D + 1),
                                                adj8[:, j, t * P:(t + 1) * P].bitcast(FP8),
                                                g[:, j, :, :, D + 1:C].rearrange("p e q c -> p (e q) c"),
                                                start=(j == 0), stop=(j == T - 1))
                    if k % 2 == 1:
                        last.then_inc(sd_done, 1)

            def transpose_pair(src, n, k):
                if n >= 2 or not isinstance(n, int):
                    pe.wait_ge(xt_copied, n - 1)
                nc.tensor.transpose(bank[6 + k % 2][:, 0:P], src[:, 2 * k:2 * k + 2, :].rearrange("p a f -> p (a f)"),
                                    ident[:, :]).then_inc(xt_done, 1)

            def add_product(w, n, k, first):
                pe.wait_ge(xt_copied, n + 1)
                nc.tensor.matmul(bank[k // 4][:, k % 4 * P:(k % 4 + 1) * P], xt2[:, k % 2, :], w,
                                 start=(first and k % 4 == 0), stop=False, skip_group_check=True).then_inc(y_added, 1)

            def spmm_tile(it, n):
                pe.wait_ge(sp_free, n + it + 1)
                pe.sem_inc(pe_passed, 1)
                for jt in range(T):
                    last = nc.tensor.matmul(bank[4 + it % 2][:, 0:3 * F], adj8[:, jt, it * P:(it + 1) * P].bitcast(FP8),
                                            parts[:, jt, :, :].rearrange("p q f -> p (q f)"), start=(jt == 0), stop=(jt == T - 1))
                last.then_inc(sp_done, 1)

            pe.wait_ge(terms_ready, 1)
            pe.wait_ge(w2_loaded, 32)
            for k in range(TP):
                transpose_pair(t_cur, k, k)
                add_product(w2_d[:, 0, :], k, k, True)

            def cheb_pass(p, w):
                pe.wait_ge(terms_ready, p + 1)
                for k in range(TP + 2):
                    if k < TP:
                        spmm_tile(2 * k, T * p)
                        spmm_tile(2 * k + 1, T * p)
                    if k >= 2:
                        add_product(w, TP * p + TP + k - 2, k - 2, False)
                    if 1 <= k <= TP:
                        pe.wait_ge(new_ready, TP * p + k)
                        transpose_pair(t_new, TP * p + TP + k - 1, k - 1)

            with pe.Fori(0, K - 2) as p:
                cheb_pass(p, w2_d[:, bass.ds(p + 1, 1), :].rearrange("p a n -> p (a n)"))
            cheb_pass(K - 2, w2_d[:, K - 1, :])
            pe.wait_ge(terms_ready, K)
            for it in range(T):
                spmm_tile(it, T * (K - 1))

        @block.vector
        def _(dve):
            chain = Chain(dve, dve_did)
            all_stat, all_root = stat, root
            v = nc.vector
            for buf in (w0_d[:, :], w1_d[:, :, :], wsn[:, :]):
                chain(v.memset(buf, 0.0))
            chain(v.memset(epsc[:, :], EPS))
            chain(v.memset(coef[:, 0:1], 1.0))
            chain(v.memset(coef[:, 1:K], 2.0))
            chain.wait()
            dve.sem_inc(w_zeroed, 1)
            v.memset(zeros, 0.0).then_inc(zero_ready, 1)

            dve.wait_ge(w_loaded, 16 * 8)
            att_b = g_val[:, 0:4, :, :].rearrange("p t e c -> p (t e c)")
            for m in range(2):
                for e in range(2):
                    rows = slice(e * F, (e + 1) * F)
                    tmp = g_res[rows, 0:2, :, :].rearrange("p t e c -> p (t e c)")[:, 0:F]
                    chain.do(v.tensor_tensor(tmp, w1_d[rows, e, 0:F], att_b[rows, m * F:(m + 1) * F], ALU.mult))
                    chain.do(v.tensor_reduce(w1_d[rows, e, F + m * H:F + (m + 1) * H],
                                             tmp.rearrange("p (h d) -> p h d", d=D), AX_X, ALU.add))
                    if m == 0:
                        chain.do(v.tensor_copy(wsn[rows, e * H:(e + 1) * H], w1_d[rows, e, F:F + H]))
            dve.sem_inc(w1_ready, 1)

            for k in range(TP):
                dve.wait_ge(prod_done, k + 1)
                v.tensor_copy(xw[:, 2 * k:2 * k + 2, :].rearrange("p a f -> p (a f)"), bank[6 + k % 2][:, 0:2 * F]).then_inc(prod_copied, 1)
            dve.wait_ge(prod_copied, TP)
            dve.wait_ge(prod_done, TP + 4)

            def split(dst, val, res):
                chain.do(v.tensor_copy(dst[0], val))
                chain.do(v.tensor_tensor(res, val, dst[0], ALU.subtract))
                chain.do(v.tensor_copy(dst[1], res))
                chain.do(v.tensor_tensor(res, res, dst[1], ALU.subtract))
                return v.tensor_copy(dst[2], res)

            def cast_rows(j, r, n):
                dve.wait_ge(stage_loaded[r % 2], 16 * n)
                dve.wait_ge(rows_free, j + 1)
                v.tensor_scalar(row_buf[r].bitcast(U8), stage[r % 2], ONE_FP8, 0.0, ALU.mult, ALU.add,
                                accum_out=deg[:, bass.ds(j, 1)]).then_inc(stage_read_dve, 1)

            def inverse_roots(j):
                dve.wait_ge(root_ready, j + 2)
                v.reciprocal(dinv[:, bass.ds(j, 2)], root[:, bass.ds(j, 2)]).then_inc(dinv_ready, 2)

            cast_rows(0, 0, 1)
            with dve.Fori(0, T // 4 - 1) as i:
                for r in range(1, 5):
                    cast_rows(4 * i + r, r % 4, 2 * i + r // 2 + 1)
                    if r % 2 == 0:
                        inverse_roots(4 * i + r - 2)
            for r in range(1, 4):
                cast_rows(T - 4 + r, r, HALF - 2 + r // 2 + 1)
                if r % 2 == 0:
                    inverse_roots(T - 6 + r)
            inverse_roots(T - 2)
            dve.wait_ge(dinv_ready, T)

            norms = [0]

            def layer_norm(dst, val, tmp, t0=0, t1=T):
                norms[0] += 1
                n, stat, root = norms[0], all_stat[:, t0:t1], all_root[:, t0:t1]
                chain.do(v.tensor_reduce(stat[:, :], val, AX_X, ALU.add))
                chain.do(v.tensor_scalar(stat[:, :], stat[:, :], 1.0 / F, None, ALU.mult))
                chain.do(v.tensor_tensor(val, val, bcast(stat[:, :], F), ALU.subtract))
                chain.do(v.tensor_tensor(tmp, val, val, ALU.mult))
                v.tensor_reduce(stat[:, :], tmp, AX_X, ALU.add).then_inc(var_ready, 1)
                dve.wait_ge(std_ready, n)
                chain.do(v.reciprocal(stat[:, :], root[:, :]))
                return v.tensor_tensor(dst, val, bcast(stat[:, :], F), ALU.mult)

            dve.wait_ge(rows_free, T + 4)
            for b in range(4):
                chain(v.tensor_tensor(work[:, 8 * b:8 * b + 8, :], bank[b][:, :].rearrange("p (t f) -> p t f", f=F),
                                      xw[:, 8 * b:8 * b + 8, :], ALU.add))
            chain.wait()
            chain.do(v.tensor_tensor(work, work, bcast(dinv[:, :], F), ALU.mult))
            chain.do(v.tensor_tensor(work, work, b0_b[:, :].unsqueeze(1).to_broadcast([P, T, F]), ALU.add))
            chain.do(v.scalar_tensor_tensor(work, work, 0.0, feat[:, :, :], ALU.max, ALU.add))
            layer_norm(x1, work, x1).then_inc(x1_ready, 1)

            for k in range(TP):
                dve.wait_ge(prod_done, TP + 4 + k + 1)
                pr2 = bank[6 + k % 2][:, 0:2 * FN].rearrange("p (a n) -> p a n", a=2)
                chain(v.tensor_copy(feat[:, 2 * k:2 * k + 2, :], pr2[:, :, 0:F]))
                v.tensor_copy(fac[:, 0:2, 2 * k:2 * k + 2, :], pr2[:, :, F:FN].rearrange("p a (m h) -> p m a h", m=2)).then_inc(prod_copied, 1)
            dve.wait_ge(prod_copied, 2 * TP)
            chain.wait()
            s_f, n_f = fac[:, 0, :, :], fac[:, 1, :, :]
            chain(v.tensor_scalar(n_cols[:, 0, :, :].rearrange("p h t -> p t h"), n_f, -1.0, None, ALU.mult))
            chain(v.tensor_scalar(n_cols[:, 1, :, :].rearrange("p h t -> p t h"), n_f, STEP, None, ALU.mult))
            v.tensor_reduce(nmax[:, 0, :], n_f.rearrange("p t h -> p h t"), AX_X, ALU.max).then_inc(nmax_part, 1)
            dve.wait_ge(nmax_ready, 1)
            top = nmax[:, 1, :].unsqueeze(1).to_broadcast([P, T, H])
            chain(v.tensor_tensor(fac[:, 0, :, :], s_f, top, ALU.add))
            chain(v.tensor_tensor(fac[:, 1, :, :], n_f, top, ALU.subtract))
            chain.wait()
            chain(v.tensor_scalar(fac[:, 2, :, :], fac[:, 0, :, :], 0.0, -(1.0 - SLOPE), ALU.max, ALU.mult))
            chain(v.tensor_scalar(fac[:, 3, :, :], fac[:, 1, :, :], SLOPE, None, ALU.mult))
            chain.wait()
            v.tensor_scalar(fac[:, 0, :, :], fac[:, 0, :, :], 0.0, 1.0 - SLOPE, ALU.min, ALU.mult).then_inc(exp_in, 1)

            mine_of = [on_dve(k) for k in range(STEPS)]
            nd, na = sum(mine_of), STEPS - sum(mine_of)
            dve.wait_ge(srow_copied, 4)

            def evac_head(pr, e):
                dve.wait_ge(sd_done, T * pr + HALF * (e + 1))
                nb = -(-T // PER_BANK)
                for b in range(nb):
                    t0, t1 = b * PER_BANK, min(T, (b + 1) * PER_BANK)
                    ins = v.tensor_reduce(r_h[:, e, t0:t1, :], bank[b][:, 0:(t1 - t0) * C3].rearrange("p (t q c) -> p t c q", q=3, c=C), AX_X, ALU.add)
                    if b < nb - 1:
                        chain(ins)
                chain.wait()
                ins.then_inc(acc_free, 1)

            def evac_sd(pr, t):
                dve.wait_ge(sd_done, T * pr + t + 1)
                v.tensor_reduce(s_d[:, t, :, :], bank[4 + t % 2][:, 0:C3].rearrange("p (e q c) -> p e c q", e=2, q=3), AX_X, ALU.add)\
                    .then_inc(sd_free, 1)

            def conj(pr, k):
                if mine_of[k]:
                    dve.wait_ge(cmp_dve, nd * pr + sum(mine_of[:k + 1]))
                else:
                    dve.wait_ge(cmp_act, na * pr + (k + 1 - sum(mine_of[:k + 1])))
                m32 = mask[k % RING].bitcast(I32)
                a32 = adj8[:, k % T, :].bitcast(I32)
                v.tensor_tensor(m32, m32, a32, ALU.bitwise_and).then_inc(mask_ready, 1)

            first = mine_of.index(True)

            def compare(pr, k):
                e = k // T
                if k % T == mine_of[e * T:].index(True):
                    dve.wait_ge(row_loaded[e], 16 * pr + 16)
                dve.wait_ge(mask_free, STEPS * pr + k + 1)
                v.tensor_scalar(mask[k % RING].bitcast(U8), s_row[e], n_cur[:, k:k + 1], ONE_FP8, ALU.is_gt, ALU.mult)\
                    .then_inc(cmp_dve, 1)

            def finish(pr):
                for t in range(T - 2, T):
                    evac_sd(pr, t)
                evac_head(pr, 1)
                dve.wait_ge(acc_free, 2 * pr + 3)
                dve.wait_ge(sd_free, T * pr + T + 2)
                dve.sem_inc(sums_ready, 1)

            def begin(pr, last):
                v.tensor_copy(cols[:, :, :], n_cols[:, :, bass.ds(2 * pr, 2), :].rearrange("p m h t -> p m (h t)")).then_inc(cols_ready, 1)
                dve.wait_ge(cols_ready, pr + 1)
                compare(pr, first)
                if last is not None:
                    finish(last)
                dve.wait_ge(g_made, pr + 1)
                v.tensor_copy(aux[:, 0:T * C3].bitcast(BF16), aux[:, T * C3:2 * T * C3].bitcast(BF16)).then_inc(g_loaded, 1)

            def steps(pr):
                for k in range(STEPS + 1):
                    if k < STEPS and mine_of[k] and k != first:
                        compare(pr, k)
                    if k >= 1:
                        conj(pr, k - 1)
                    if k == 5:
                        dve.wait_ge(sums_used, pr + 1)
                    if k in (T, STEPS):
                        dve.wait_ge(cmp_dve, nd * pr + sum(mine_of[:k]))
                        dve.sem_inc(row_free[k // T - 1], 1)
                    if k >= 5 and k % 2 == 1:
                        evac_sd(pr, (k - 5) // 2)
                    if k == T + 1:
                        evac_head(pr, 0)

            begin(0, None)
            with dve.Fori(0, PAIRS - 1) as pr:
                chain.body(pr, 2 * 3)
                steps(pr)
                begin(pr + 1, pr)
                chain.end(PAIRS - 1)
            steps(PAIRS - 1)
            finish(PAIRS - 1)

            dve.wait_ge(sums_used, PAIRS + 1)
            chain.do(v.memset(w2_d, 0.0))
            dve.sem_inc(w2_zeroed, 1)
            chain.do(v.reciprocal(den[:, :, :], den[:, :, :]))
            f4 = feat[:, :, :].rearrange("p t (h d) -> p t h d", d=D)
            chain.do(v.tensor_tensor(f4, f4, den[:, :, :].unsqueeze(3).to_broadcast([P, T, H, D]), ALU.mult))
            chain.do(v.tensor_tensor(feat[:, :, :], feat[:, :, :], b1_b[:, :].unsqueeze(1).to_broadcast([P, T, F]), ALU.add))
            dve.wait_ge(x1_back, 16)
            chain.do(v.scalar_tensor_tensor(feat[:, :, :], feat[:, :, :], 0.0, x1, ALU.max, ALU.add))
            dve.wait_ge(row_free[1], 2 * PAIRS + 2)
            chain.do(layer_norm(feat[:, :, :], feat[:, :, :], work))

            def all_parts(val, res, dst):
                return split([dst[:, :, q, :] for q in range(3)], val, res)

            chain.do(v.tensor_copy(t_cur, feat[:, :, :]))
            chain(v.memset(t_old, 0.0))
            chain.do(all_parts(t_cur, big2, parts))
            dve.sem_inc(terms_ready, 1)
            res = aux[:, 0:4 * F].rearrange("p (a f) -> p a f", f=F)
            FLAT = 3 * F

            def new_pair(p, k, scale):
                for a in range(2):
                    dve.wait_ge(sp_done, T * p + 2 * k + a + 1)
                    v.tensor_reduce(res[:, a, :], bank[4 + a][:, 0:3 * F].rearrange("p (q f) -> p f q", q=3), AX_X, ALU.add)\
                        .then_inc(sp_free, 1)
                if k == 0:
                    dve.wait_ge(xt_done, TP * p + TP)
                    dve.wait_ge(shifted, 2 * p + 1)
                dve.wait_ge(sp_free, T * p + 2 * k + 4)
                v.scalar_tensor_tensor(t_new[:, 2 * k:2 * k + 2, :], res[:, 0:2, :], scale, t_old[:, 2 * k:2 * k + 2, :],
                                       ALU.mult, ALU.subtract).then_inc(new_ready, 1)
                dve.wait_ge(new_ready, TP * p + k + 1)

            with dve.Fori(0, K - 2) as p:
                chain.body(p, TP * 5 + 1)
                for k in range(TP):
                    new_pair(p, k, coef[:, bass.ds(p, 1)])
                    dst = parts_new if k < TP - 1 else parts
                    chain.do(split([dst[:, 2 * k:2 * k + 2, q, :] for q in range(3)], t_new[:, 2 * k:2 * k + 2, :], res[:, 2:4, :]))
                chain.do(v.tensor_copy(parts[:, 0:T - 2, :, :], parts_new[:, 0:T - 2, :, :]))
                dve.sem_inc(terms_ready, 1)
                chain.end(K - 2)

            def x3_tiles(b):
                dve.wait_ge(y_added, TP * (K - 1) + 4 * b + 4)
                t0, t1 = 8 * b, 8 * b + 8
                x3, tmp = feat[:, t0:t1, :], big2[:, 8:16, :]
                chain.do(v.tensor_tensor(x3, bank[b][:, :].rearrange("p (t f) -> p t f", f=F), x3, ALU.add))
                chain.do(layer_norm(x3, x3, tmp, t0, t1))
                dst = parts_new if b < T // 8 - 1 else parts
                chain.do(split([dst[:, t0:t1, q, :] for q in range(3)], x3, tmp))

            for k in range(TP):
                new_pair(K - 2, k, 2.0)
                if k % 4 == 1 and k >= 5:
                    x3_tiles((k - 5) // 4)
            x3_tiles(TP // 4 - 1)
            chain.do(v.tensor_copy(parts[:, 0:T - 8, :, :], parts_new[:, 0:T - 8, :, :]))
            dve.sem_inc(terms_ready, 1)

            for m in range(T // L3G):
                t0, t1 = L3G * m, L3G * (m + 1)
                x3, ax, y = feat[:, t0:t1, :], t_new[:, t0:t1, :], t_old[:, t0:t1, :]
                chain.do(v.tensor_scalar(y, x3, -0.1, 1.0, ALU.mult, ALU.add))
                for it in range(t0, t1):
                    dve.wait_ge(sp_done, T * (K - 1) + it + 1)
                    v.tensor_reduce(t_new[:, it, :], bank[4 + it % 2][:, 0:3 * F].rearrange("p (q f) -> p f q", q=3), AX_X, ALU.add)\
                        .then_inc(sp_free, 1)
                dve.wait_ge(sp_free, T * (K - 1) + t1 + 2)
                chain.do(v.tensor_tensor(ax, ax, x3, ALU.mult))
                chain.do(v.tensor_reduce(stat[:, t0:t1], ax, AX_X, ALU.add))
                chain.do(v.tensor_scalar(stat[:, t0:t1], stat[:, t0:t1], 0.01, None, ALU.mult))
                chain.do(v.tensor_tensor(y, y, bcast(stat[:, t0:t1], F), ALU.subtract))
                chain.do(v.tensor_tensor(y, y, x3, ALU.add))
                layer_norm(x3, y, ax, t0, t1).then_inc(out_ready, 1)


_INS = ['x', 'adj', 'L0_gnn_W', 'L0_gnn_b', 'L1_gnn_W', 'L1_gnn_att_self', 'L1_gnn_att_neigh', 'L1_gnn_bias', 'L2_gnn_weight']


def kernel(**inputs):
    import numpy as _np
    import concourse.bacc as _bacc
    from concourse import mybir as _mybir
    from concourse.bass_utils import run_bass_kernel_spmd as _run

    nc = _bacc.Bacc("TRN2", target_bir_lowering=False, num_devices=1, dynamic_dma_scratch_size=1024)
    arrays, args = {}, []
    for name in _INS:
        a = _np.ascontiguousarray(inputs[name])
        arrays[f"in_{name}_dram"] = a
        args.append(nc.dram_tensor(f"in_{name}_dram", a.shape, _mybir.dt.from_np(a.dtype), kind="ExternalInput").ap())
    n, f = inputs["x"].shape
    args.append(nc.dram_tensor("out_0_dram", (n, f), _mybir.dt.float32, kind="ExternalOutput").ap())
    args.append(nc.dram_tensor("scratch_rows", (8, n), _mybir.dt.float32, kind="Internal").ap())
    args.append(nc.dram_tensor("scratch_x", (n, f), _mybir.dt.float32, kind="Internal").ap())
    graph_layers(nc, *args)
    r = _run(nc, [arrays], core_ids=[0])
    return r.results[0]["out_0_dram"]
```

```python
from contextlib import ExitStack

import concourse.bass as bass
from concourse import mybir

P = 128
F32, BF16 = mybir.dt.float32, mybir.dt.bfloat16
FP8, U8, I32 = mybir.dt.float8e4, mybir.dt.uint8, mybir.dt.int32
ALU = mybir.AluOpType
ACT = mybir.ActivationFunctionType
AX_X = mybir.AxisListType.X
RMAX = bass.bass_isa.ReduceOp.max

ONE_FP8 = 56.0
STEP = float(2.0 ** 60)
SLOPE = 0.2
EPS = 1e-5
RING = 4
DVE_SHARE = 26, 64


def on_dve(k):
    part, whole = DVE_SHARE
    return (k + 1) * part // whole > k * part // whole


class Chain:

    def __init__(self, eng, sem, passed=None):
        self.passed = passed
        self.eng, self.sem, self.n, self.loop = eng, sem, 0, 0

    def __call__(self, ins):
        ins.then_inc(self.sem, 1)
        self.n += 1

    def wait(self):
        self.eng.wait_ge(self.sem, self.loop + self.n)
        if self.passed is not None:
            self.eng.sem_inc(self.passed, 1)

    def do(self, ins):
        self(ins)
        self.wait()

    def body(self, i, per):
        self.start, self.per, self.loop = self.n, per, i * per

    def end(self, count):
        assert self.n - self.start == self.per, (self.n - self.start, self.per)
        self.n, self.loop = self.start + self.per * count, 0


def graph_layers(nc, x, adj, w0, b0, w1, att_self, att_neigh, bias1, w2, out, sc_rows, sc_x):
    N, F = x.shape
    H, D = att_self.shape
    K = w2.shape[0]
    T = N // P
    TP = T // 2
    PAIRS = H // 2
    C = 2 * (D + 1)
    C3 = 3 * C
    PER_BANK = 512 // C3
    FN = F + 2 * H
    STEPS = 2 * T
    assert (N, F, H * D) == (4096, 64, F) and T % PER_BANK <= PER_BANK

    x_t = x.rearrange("(t p) f -> p t f", p=P)
    out_t = out.rearrange("(t p) f -> p t f", p=P)
    sc_x_t = sc_x.rearrange("(p t) f -> p t f", p=P)
    adj_t = adj.rearrange("(t p) n -> t p n", p=P)

    with ExitStack() as ctx:
        def sb(name, shape, dt=F32):
            return ctx.enter_context(nc.sbuf_tensor(name, shape, dt))

        def sem(name):
            return ctx.enter_context(nc.semaphore(name))

        adj8 = sb("adj8", [P, T, N], U8)
        big = sb("big", [P, 3 * N])
        feat = sb("feat", [P, T, F])
        aux = sb("aux", [P, 2 * T * C3], F32)
        r_h = sb("r_h", [P, 2, T, C])
        s_d = sb("s_d", [P, T, 2, D + 1])
        den = sb("den", [P, T, H])
        fac = sb("fac", [P, 4, T, H])
        n_cols = sb("n_cols", [P, 2, H, T])
        cols = sb("cols", [P, 2, 2 * T])
        n_cur, k_cur = cols[:, 0, :], cols[:, 1, :]
        g_val = sb("g_val", [P, T, 2, C])
        g_res = sb("g_res", [P, T, 2, C])
        ident = sb("ident", [P, P])
        b0_b = sb("b0_b", [P, F])
        b1_b = sb("b1_b", [P, F])
        deg2 = sb("deg2", [P, 2, T])
        deg = sb("deg", [P, T])
        dinv = sb("dinv", [P, T])
        root = sb("root", [P, T])
        stat = sb("stat", [P, T])
        nmax = sb("nmax", [P, 2, H])
        coef = sb("coef", [P, K])
        epsc = sb("epsc", [P, 1])

        bank = [ctx.enter_context(nc.psum_tensor(f"bank{b}", [P, 512], F32)) for b in range(8)]

        NH = N // 2
        stage = [big[:, NH * q:NH * (q + 1)] for q in range(4)]
        row_buf = [big[:, 2 * N + N // 4 * r:2 * N + N // 4 * (r + 1)] for r in range(4)]
        zeros = row_buf[0].bitcast(BF16)[:, 0:512]
        x_tr = adj8[:, T - 4:T, :].rearrange("p a n -> p (a n)").bitcast(F32)[:, 0:TP * P]
        xw = aux[:, 0:T * F].rearrange("p (t f) -> p t f", f=F)
        z_res = aux[:, T * F:T * F + 2 * F].rearrange("p (a f) -> p a f", f=F)
        z_part = aux[:, T * F + 2 * F:T * F + 5 * F].bitcast(BF16).rearrange("p (u q f) -> p u q f", u=2, q=3)
        x1 = big[:, N:N + T * F].rearrange("p (t f) -> p t f", f=F)
        work = big[:, 0:T * F].rearrange("p (t f) -> p t f", f=F)
        x1_b = work
        x1_tr = big[:, 2 * N:2 * N + TP * P]
        s_rows = big[0:2 * H, T * F:T * F + TP * P]
        s_row = [big[:, 0:N], big[:, N:2 * N]]
        mask = [big[:, 2 * N + N // RING * r:2 * N + N // RING * (r + 1)] for r in range(RING)]
        g = aux[:, 0:T * C3].bitcast(BF16).rearrange("p (t e q c) -> p t e q c", t=T, e=2, q=3)
        g_next = aux[:, T * C3:2 * T * C3].bitcast(BF16).rearrange("p (t e q c) -> p t e q c", t=T, e=2, q=3)
        TF = T * F

        early = r_h[:, :, :, :].rearrange("p e t c -> p (e t c)")
        w0_d = early[:, 0:2 * F]
        w1_d = early[:, 2 * F:2 * F + 2 * FN].rearrange("p (e n) -> p e n", e=2)
        wsn = early[:, 4 * F + 2 * FN:4 * F + 2 * FN + 2 * H]
        w2_d = g_res[:, :, :, :].rearrange("p t e c -> p (t e c)")[:, 0:K * 2 * F].rearrange("p (k o) -> p k o", k=K)
        xt2 = g_val[:, :, :, :].rearrange("p t e c -> p (t e c)")[:, 0:2 * P].rearrange("p (a c) -> p a c", a=2)
        xt8 = g_val[:, :, :, :].rearrange("p t e c -> p (t e c)")[:, 0:8 * P].rearrange("p (a c) -> p a c", a=2)

        def term(k):
            return big[:, k * TF:(k + 1) * TF].rearrange("p (t f) -> p t f", f=F)
        t_cur, t_old, t_new = term(0), term(1), term(2)
        parts = big[:, 3 * TF:3 * TF + 3 * TF // 2].bitcast(BF16).rearrange("p (t q f) -> p t q f", q=3, f=F)
        parts_new = big[:, 3 * TF + 3 * TF // 2:6 * TF].bitcast(BF16).rearrange("p (t q f) -> p t q f", q=3, f=F)
        res2 = aux[:, 0:2 * F].rearrange("p (a f) -> p a f", f=F)
        big2 = aux[:, 0:T * F].rearrange("p (t f) -> p t f", f=F)

        x_loaded = [sem("x0_loaded"), sem("x1_loaded")]
        w_loaded = sem("w_loaded")
        w_zeroed = sem("w_zeroed")
        w_issued = sem("w_issued")
        stage_loaded = [sem(f"stage{q}_loaded") for q in range(4)]
        deg_ready = sem("deg_ready")
        stage_read_act = sem("stage_read_act")
        stage_read_dve = sem("stage_read_dve")
        const_ready = sem("const_ready")
        dve_did = sem("dve_did")
        act_passed = sem("act_passed")
        pe_passed = sem("pe_passed")
        pool_passed = sem("pool_passed")
        act_did = sem("act_did")
        pool_did = sem("pool_did")
        tr_done = sem("tr_done")
        tr_copied = sem("tr_copied")
        prod_done = sem("prod_done")
        prod_copied = sem("prod_copied")
        zero_ready = sem("zero_ready")
        dinv_ready = sem("dinv_ready")
        root_ready = sem("root_ready")
        z_ready = sem("z_ready")
        zb_ready = sem("zb_ready")
        rows_free = sem("rows_free")
        x1_ready = sem("x1_ready")
        l0_evacuated = sem("l0_evacuated")
        centred = sem("centred")
        squared = sem("squared")
        var_ready = sem("var_ready")
        std_ready = sem("std_ready")
        w1_ready = sem("w1_ready")
        feat_done = sem("feat_done")
        feat_copied = sem("feat_copied")
        srow_done = sem("srow_done")
        srow_copied = sem("srow_copied")
        srow_stored = sem("srow_stored")
        x1_stored = sem("x1_stored")
        nmax_part = sem("nmax_part")
        nmax_ready = sem("nmax_ready")
        exp_in = sem("exp_in")
        exp_out = sem("exp_out")
        cols_ready = sem("cols_ready")
        row_loaded = [sem("row0_loaded"), sem("row1_loaded")]
        row_free = [sem("row0_free"), sem("row1_free")]
        cmp_act = sem("cmp_act")
        cmp_dve = sem("cmp_dve")
        mask_ready = sem("mask_ready")
        mask_free = sem("mask_free")
        acc_free = sem("acc_free")
        sd_done = sem("sd_done")
        sd_free = sem("sd_free")
        g_made = sem("g_made")
        g_loaded = sem("g_loaded")
        sums_ready = sem("sums_ready")
        sums_used = sem("sums_used")
        x1_back = sem("x1_back")
        den_inverted = sem("den_inverted")
        divided = sem("divided")
        w2_zeroed = sem("w2_zeroed")
        old_zeroed = sem("old_zeroed")
        w2_loaded = sem("w2_loaded")
        terms_ready = sem("terms_ready")
        x2_ready = sem("x2_ready")
        rest_ready = sem("rest_ready")
        rest2_ready = sem("rest2_ready")
        part_cast = [sem(f"part{q}_cast") for q in range(3)]
        cur_ready = sem("cur_ready")
        shifted = sem("shifted")
        sp_done = sem("sp_done")
        sp_free = sem("sp_free")
        new_ready = sem("new_ready")
        xt_done = sem("xt_done")
        xt_copied = sem("xt_copied")
        y_added = sem("y_added")
        out_ready = sem("out_ready")
        out_stored = sem("out_stored")
        block = ctx.enter_context(nc.Block())

        SUM_BANKS = (2, 3, 0, 1), (6, 7, 0, 1)
        SP_BANKS = 4, 5, 7
        L3_BANKS = 4, 5, 7, 0, 1, 2
        HALF = T // 2
        GROUPS = T // 8
        L3_STEPS = [(t, t + 4) for t in range(0, T - 4, 4)] + [(T - 4, T - 2), (T - 2, T)]

        def bcast(ap2, n):
            return ap2.unsqueeze(2).to_broadcast([P, ap2.shape[1], n])

        def prepare(eng, chain, pr, dst):
            fh = feat[:, :, bass.ds(pr * 2 * D, 2 * D)].rearrange("p t (e d) -> p t e d", e=2)
            for m, o in ((1, 0), (3, D + 1)):
                fm = fac[:, m, :, bass.ds(pr * 2, 2)]
                chain(eng.tensor_tensor(g_val[:, :, :, o:o + D], fh, fm.unsqueeze(3).to_broadcast([P, T, 2, D]), ALU.mult))
                chain(eng.tensor_copy(g_val[:, :, :, o + D], fm))
            chain.wait()
            chain.do(eng.tensor_copy(dst[:, :, :, 0, :], g_val[:, :, :, :]))
            chain.do(eng.tensor_tensor(g_res[:, :, :, :], g_val[:, :, :, :], dst[:, :, :, 0, :], ALU.subtract))
            chain.do(eng.tensor_copy(dst[:, :, :, 1, :], g_res[:, :, :, :]))
            chain.do(eng.tensor_tensor(g_val[:, :, :, :], g_res[:, :, :, :], dst[:, :, :, 1, :], ALU.subtract))
            return eng.tensor_copy(dst[:, :, :, 2, :], g_val[:, :, :, :])

        def combine(eng, chain, pr):
            a = fac[:, 0, :, bass.ds(pr * 2, 2)]
            c = fac[:, 2, :, bass.ds(pr * 2, 2)]
            for e in range(2):
                mb, md = r_h[:, e, :, 0:D + 1], r_h[:, e, :, D + 1:C]
                chain(eng.tensor_tensor(md, s_d[:, :, e, :], md, ALU.subtract))
                chain(eng.tensor_tensor(mb, mb, bcast(a[:, :, e], D + 1), ALU.mult))
            chain.wait()
            for e in range(2):
                md = r_h[:, e, :, D + 1:C]
                chain(eng.tensor_tensor(md, md, bcast(c[:, :, e], D + 1), ALU.mult))
            chain.wait()
            for e in range(2):
                mb, md = r_h[:, e, :, 0:D + 1], r_h[:, e, :, D + 1:C]
                chain(eng.tensor_tensor(feat[:, :, bass.ds((pr * 2 + e) * D, D)], mb[:, :, 0:D], md[:, :, 0:D], ALU.add))
                chain(eng.tensor_tensor(den[:, :, bass.ds(pr * 2 + e, 1)], mb[:, :, D:D + 1], md[:, :, D:D + 1], ALU.add))
            chain.wait()

        def divide(eng, chain, h0, h1):
            f = feat[:, :, h0 * D:h1 * D]
            f4 = f.rearrange("p t (h d) -> p t h d", d=D)
            chain.do(eng.tensor_tensor(f4, f4, den[:, :, h0:h1].unsqueeze(3).to_broadcast([P, T, h1 - h0, D]), ALU.mult))
            return eng.tensor_tensor(f, f, b1_b[:, h0 * D:h1 * D].unsqueeze(1).to_broadcast([P, T, (h1 - h0) * D]), ALU.add)

        @block.sync
        def _(sp):
            for m in range(2):
                sp.dma_start(feat[:, HALF * m:HALF * (m + 1), :], x_t[:, HALF * m:HALF * (m + 1), :]).then_inc(x_loaded[m], 16)
            sp.wait_ge(w_issued, 1)
            for q in range(4):
                sp.dma_start(stage[q], adj_t[q // 2][:, q % 2 * NH:(q % 2 + 1) * NH]).then_inc(stage_loaded[q], 16)
            with sp.Fori(1, HALF) as i:
                for q in range(4):
                    sp.wait_ge(stage_read_act, 4 * i + q - 3)
                    sp.wait_ge(stage_read_dve, 4 * i + q - 3)
                    sp.dma_start(stage[q], adj_t[bass.ds(2 * i + q // 2, 1), :, q % 2 * NH:(q % 2 + 1) * NH].rearrange("a p n -> (a p) n"))\
                        .then_inc(stage_loaded[q], 16)
            def store_x1(b):
                sp.wait_ge(x1_ready, b + 1)
                sp.dma_start(sc_x_t[:, 8 * b:8 * b + 8, :], x1[:, 8 * b:8 * b + 8, :]).then_inc(x1_stored, 16)

            for b in range(3):
                store_x1(b)
            sp.wait_ge(srow_copied, 4)
            sr = sc_rows.rearrange("h (k e c) -> e h k c", e=2, c=P)
            for e in range(2):
                sp.dma_start(sr[e], s_rows[e * H:(e + 1) * H, :].rearrange("p (k c) -> p k c", c=P)).then_inc(srow_stored, 16)
            sp.wait_ge(srow_stored, 32)
            sp.dma_start(s_row[0], sc_rows[0:1, :].to_broadcast([P, N])).then_inc(row_loaded[0], 16)
            store_x1(3)
            sp.wait_ge(x1_stored, 64)
            sp.wait_ge(tr_done, 2 * GROUPS)
            sp.dma_start(s_row[1], sc_rows[1:2, :].to_broadcast([P, N])).then_inc(row_loaded[1], 16)
            with sp.Fori(1, PAIRS) as pr:
                for e in range(2):
                    sp.wait_ge(row_free[e], 2 * pr)
                    sp.dma_start(s_row[e], sc_rows[bass.ds(2 * pr + e, 1), :].to_broadcast([P, N])).then_inc(row_loaded[e], 16)
            sp.wait_ge(row_free[0], 2 * PAIRS)
            sp.dma_start(x1_b, sc_x_t).then_inc(x1_back, 16)
            sp.wait_ge(w2_zeroed, 1)
            for e in range(2):
                sp.dma_start(w2_d[e * F:(e + 1) * F, :, e * F:(e + 1) * F], w2.rearrange("k i o -> i k o")).then_inc(w2_loaded, 16)
            for m, (t0, t1) in enumerate(L3_STEPS):
                sp.wait_ge(out_ready, m + 1)
                sp.dma_start(out_t[:, t0:t1, :], feat[:, t0:t1, :]).then_inc(out_stored, 16)
            sp.wait_ge(out_stored, 16 * len(L3_STEPS))

        @block.gpsimd
        def _(pool):
            chain = Chain(pool, pool_did, pool_passed)
            pool.sem_inc(sums_used, 1)
            chain.do(nc.gpsimd.memset(ident[:, :], 0.0))
            nc.gpsimd.affine_select(out=ident[:, :], in_=ident[:, :], compare_op=ALU.not_equal, fill=1.0,
                                    base=0, pattern=[[-1, P]], channel_multiplier=1).then_inc(const_ready, 1)
            pool.wait_ge(prod_copied, GROUPS)
            with pool.Fori(0, HALF) as i:
                chain.body(i, 2 * 7)
                for u in range(2):
                    t = bass.ds(2 * i + u, 1)
                    pool.wait_ge(rows_free, 2 * i + u + 3)
                    pool.wait_ge(dinv_ready, 2 * i + u + 1)
                    pool.sem_inc(pool_passed, 1)
                    chain.do(nc.gpsimd.tensor_tensor(xw[:, t, :], xw[:, t, :], dinv[:, t].unsqueeze(2).to_broadcast([P, 1, F]), ALU.mult))
                    chain.do(nc.gpsimd.tensor_copy(z_part[:, u, 0:1, :], xw[:, t, :]))
                    chain.do(nc.gpsimd.tensor_tensor(z_res[:, 0:1, :], xw[:, t, :], z_part[:, u, 0:1, :], ALU.subtract))
                    chain.do(nc.gpsimd.tensor_copy(z_part[:, u, 1:2, :], z_res[:, 0:1, :]))
                    chain.do(nc.gpsimd.tensor_tensor(z_res[:, 1:2, :], z_res[:, 0:1, :], z_part[:, u, 1:2, :], ALU.subtract))
                    nc.gpsimd.tensor_copy(z_part[:, u, 2:3, :], z_res[:, 1:2, :]).then_inc(z_ready, 1)
                    chain.do(nc.gpsimd.tensor_tensor(xw[:, t, :], xw[:, t, :], dinv[:, t].unsqueeze(2).to_broadcast([P, 1, F]), ALU.mult))
                    chain.do(nc.gpsimd.tensor_tensor(xw[:, t, :], xw[:, t, :], b0_b[:, :].unsqueeze(1), ALU.add))
                chain.end(HALF)
            pool.sem_inc(zb_ready, 1)
            pool.wait_ge(nmax_part, 1)
            nc.gpsimd.partition_all_reduce(nmax[:, 1, :], nmax[:, 0, :], P, RMAX).then_inc(nmax_ready, 1)

            pool.wait_ge(exp_out, 1)
            with pool.Fori(0, PAIRS - 1) as pr:
                chain.body(pr, 8 + 10)
                pool.wait_ge(g_loaded, pr + 1)
                prepare(nc.gpsimd, chain, pr + 1, g_next).then_inc(g_made, 1)
                pool.wait_ge(sums_ready, pr + 1)
                combine(nc.gpsimd, chain, pr)
                pool.sem_inc(sums_used, 1)
                chain.end(PAIRS - 1)
            nc.gpsimd.memset(w2_d, 0.0).then_inc(w2_zeroed, 1)
            pool.wait_ge(den_inverted, 1)
            divide(nc.gpsimd, chain, 0, H - 2).then_inc(divided, 1)
            pool.wait_ge(row_free[0], 2 * PAIRS)
            nc.gpsimd.memset(t_old, 0.0).then_inc(old_zeroed, 1)

        @block.scalar
        def _(act):
            chain = Chain(act, act_did, act_passed)
            act.wait_ge(w_zeroed, 1)
            for e in range(2):
                rows = slice(e * F, (e + 1) * F)
                act.dma_start(w0_d[rows, e * F:(e + 1) * F], w0).then_inc(w_loaded, 16)
                act.dma_start(w1_d[rows, e, 0:F], w1).then_inc(w_loaded, 16)
            act.dma_start(b0_b[:, :], b0.rearrange("(a n) -> a n", a=1).to_broadcast([P, F])).then_inc(w_loaded, 16)
            act.dma_start(b1_b[:, :], bias1.rearrange("h d -> (h d)").rearrange("(a n) -> a n", a=1).to_broadcast([P, F])).then_inc(w_loaded, 16)
            for m, att in enumerate((att_self, att_neigh)):
                act.dma_start(g_val[:, 0:4, :, :].rearrange("p t e c -> p (t e c)")[:, m * F:(m + 1) * F],
                              att.rearrange("h d -> (h d)").rearrange("(a n) -> a n", a=1).to_broadcast([P, F])).then_inc(w_loaded, 16)

            act.sem_inc(w_issued, 1)
            chain.do(nc.scalar.activation(root[:, 0:1], epsc[:, 0:1], ACT.Sqrt))

            def copy_transposed(dst, g, n):
                act.wait_ge(tr_done, n)
                nc.scalar.activation(dst[:, 4 * g * P:4 * (g + 1) * P], bank[4 + g % 2][:, :], ACT.Copy).then_inc(tr_copied, 1)

            for grp in range(GROUPS):
                copy_transposed(x_tr, grp, grp + 1)
            act.wait_ge(prod_done, GROUPS)
            def rows8(j, u, n):
                for c in range(2):
                    act.wait_ge(stage_loaded[2 * u + c], 16 * n)
                    nc.scalar.activation(adj8[:, bass.ds(j, 1), c * NH:(c + 1) * NH].rearrange("p a n -> p (a n)"), stage[2 * u + c],
                                         ACT.Copy, scale=ONE_FP8).then_inc(stage_read_act, 1)

                act.wait_ge(deg_ready, j + 1)
                nc.scalar.activation(root[:, bass.ds(j, 1)], deg[:, bass.ds(j, 1)], ACT.Sqrt, bias=1.0, scale=1.0 / ONE_FP8).then_inc(root_ready, 1)

            with act.Fori(0, HALF) as i:
                for u in range(2):
                    rows8(2 * i + u, u, i + 1)

            def norm_root(n, t0=0, t1=T):
                act.wait_ge(var_ready, n)
                nc.scalar.activation(root[:, t0:t1], stat[:, t0:t1], ACT.Sqrt, bias=epsc[:, 0:1], scale=1.0 / F).then_inc(std_ready, 1)

            def square(src, dst, n, b):
                act.wait_ge(centred, n)
                nc.scalar.activation(dst[:, 8 * b:8 * b + 8, :], src[:, 8 * b:8 * b + 8, :], ACT.Square).then_inc(squared, 1)

            def evacuate(b):
                for t in range(8 * b, 8 * b + 8):
                    nc.scalar.activation(work[:, t, :], bank[b][:, t % 8 * F:(t % 8 + 1) * F], ACT.Copy, scale=dinv[:, t:t + 1])\
                        .then_inc(l0_evacuated, 1)

            act.wait_ge(stage_read_dve, 2 * T)
            act.wait_ge(dinv_ready, T)
            act.wait_ge(rows_free, T + 4)
            evacuate(0)
            for b in range(GROUPS + 2):
                if b + 1 < GROUPS:
                    evacuate(b + 1)
                if b < GROUPS:
                    square(work, xw, b + 1, b)
                if 1 <= b <= GROUPS:
                    norm_root(b, 8 * b - 8, 8 * b)
                if 2 <= b:
                    act.wait_ge(srow_done, b - 1)
                    nc.scalar.activation(s_rows[:, (b - 2) * 512:(b - 1) * 512], bank[b - 2][0:2 * H, :], ACT.Copy).then_inc(srow_copied, 1)
                if 1 <= b <= GROUPS:
                    copy_transposed(x1_tr, b - 1, GROUPS + b)
            act.wait_ge(exp_in, 1)
            nc.scalar.activation(fac[:, :, :, :], fac[:, :, :, :], ACT.Exp).then_inc(exp_out, 1)
            chain.do(nc.scalar.activation(root[:, 0:1], epsc[:, 0:1], ACT.Sigmoid))

            na = sum(not on_dve(k) for k in range(STEPS))
            with act.Fori(0, PAIRS) as pr:
                chain.body(pr, 1)
                chain.do(nc.scalar.activation(k_cur, n_cols[:, 1, bass.ds(2 * pr, 2), :].rearrange("p h t -> p (h t)"), ACT.Copy))
                chain.end(PAIRS)
                for e in range(2):
                    act.wait_ge(row_loaded[e], 16 * pr + 16)
                    mine = [k for k in range(e * T, (e + 1) * T) if not on_dve(k)]
                    for k in mine:
                        act.wait_ge(mask_free, STEPS * pr + k + 1)
                        act.sem_inc(act_passed, 1)
                        nc.scalar.activation(mask[k % RING].bitcast(FP8), s_row[e], ACT.Sigmoid,
                                             bias=k_cur[:, k:k + 1], scale=STEP, saturate=False).then_inc(cmp_act, 1)
                    act.wait_ge(cmp_act, na * pr + sum(not on_dve(k) for k in range((e + 1) * T)))
                    act.sem_inc(row_free[e], 1)
            def copy_xt(n, k):
                act.wait_ge(xt_done, n + 1)
                nc.scalar.activation(xt2[:, k % 2, :], bank[6][:, 0:P], ACT.Copy).then_inc(xt_copied, 1)

            def cast_part(q, b, src, ready, n):
                act.wait_ge(ready, n)
                nc.scalar.activation(parts[:, 8 * b:8 * b + 8, q, :], src[:, 8 * b:8 * b + 8, :], ACT.Copy).then_inc(part_cast[q], 1)

            chain.do(nc.scalar.activation(root[:, 0:1], epsc[:, 0:1], ACT.Sqrt))

            for b in range(GROUPS + 3):
                if b < GROUPS:
                    square(feat, big2, GROUPS + b + 1, b)
                if 1 <= b <= GROUPS:
                    norm_root(GROUPS + b, 8 * b - 8, 8 * b)
                if 2 <= b <= GROUPS + 1:
                    act.wait_ge(xt_done, b - 1)
                    nc.scalar.activation(xt8[:, b % 2, :], bank[6 + b % 2][:, :], ACT.Copy).then_inc(xt_copied, 1)
                    cast_part(1, b - 2, big2, rest_ready, b - 1)
                if 3 <= b:
                    cast_part(2, b - 3, big2, rest2_ready, b - 2)
                if b == GROUPS + 1:
                    act.wait_ge(part_cast[2], GROUPS - 1)
                    act.sem_inc(terms_ready, 1)
                if 1 <= b <= GROUPS:
                    cast_part(0, b - 1, feat, x2_ready, b)
                    t0, t1 = 8 * b - 8, 8 * b
                    nc.scalar.activation(t_cur[:, t0:t1, :], feat[:, t0:t1, :], ACT.Copy).then_inc(cur_ready, 1)
            act.wait_ge(cur_ready, GROUPS)
            act.wait_ge(old_zeroed, 1)
            act.sem_inc(shifted, 1)
            for q in range(3):
                act.wait_ge(part_cast[q], GROUPS)
            act.sem_inc(terms_ready, 1)
            with act.Fori(0, K - 2) as p:
                for k in range(TP):
                    copy_xt(TP * p + GROUPS + k, k)
                act.wait_ge(new_ready, TP * p + TP)
                nc.scalar.activation(t_old, t_cur, ACT.Copy).then_inc(shifted, 1)
                act.wait_ge(shifted, 2 * p + 2)
                nc.scalar.activation(t_cur, t_new, ACT.Copy).then_inc(shifted, 1)
            for k in range(TP):
                copy_xt(TP * (K - 2) + GROUPS + k, k)
                if k % 4 == 2 and k >= 6:
                    norm_root(2 * GROUPS + k // 4, 2 * k - 12, 2 * k - 4)
            norm_root(3 * GROUPS, T - 8, T)
            for m, (t0, t1) in enumerate(L3_STEPS):
                norm_root(3 * GROUPS + m + 1, t0, t1)

        @block.tensor
        def _(pe):
            pe.sem_inc(rows_free, 4)
            pe.sem_inc(mask_free, RING)
            pe.sem_inc(acc_free, 1)
            pe.sem_inc(sd_free, 2)

            def transpose_group(src, dst, g):
                for k in range(4):
                    t = 8 * g + 2 * k
                    last = nc.tensor.transpose(dst[:, k * P:(k + 1) * P], src[:, t:t + 2, :].rearrange("p a f -> p (a f)"), ident[:, :])
                return last

            pe.wait_ge(const_ready, 1)
            for grp in range(GROUPS + 1):
                if grp < GROUPS:
                    if grp % (GROUPS // 2) == 0:
                        pe.wait_ge(x_loaded[grp // (GROUPS // 2)], 16)
                    if grp >= 2:
                        pe.wait_ge(tr_copied, grp - 1)
                    transpose_group(feat, bank[4 + grp % 2], grp).then_inc(tr_done, 1)
                if grp >= 1:
                    j = grp - 1
                    if j == 0:
                        pe.wait_ge(w_loaded, 16 * 8)
                    if j >= 2:
                        pe.wait_ge(prod_copied, j - 1)
                    pe.wait_ge(tr_copied, j + 1)
                    for k in range(4):
                        last = nc.tensor.matmul(bank[6 + j % 2][:, k * P:(k + 1) * P], x_tr[:, (4 * j + k) * P:(4 * j + k + 1) * P], w0_d[:, :],
                                                start=True, stop=True)
                    last.then_inc(prod_done, 1)

            pe.wait_ge(zero_ready, 1)
            for b in range(4):
                nc.tensor.matmul(bank[b][:, :], zeros[:, 0:P], zeros, start=True, stop=False, skip_group_check=True)\
                    .then_inc(prod_done, 1)
            with pe.Fori(0, T // 4) as i:
                for u in range(4):
                    pe.wait_ge(z_ready, 4 * i + u + 1)
                    pe.sem_inc(pe_passed, 1)
                    for it in range(T):
                        for q in range(3):
                            last = nc.tensor.matmul(bank[it // 8][:, (it % 8) * F:(it % 8 + 1) * F],
                                                    row_buf[u].bitcast(FP8)[:, it * P:(it + 1) * P], z_part[:, u % 2, q, :],
                                                    start=False, stop=False, skip_group_check=True)
                    last.then_inc(rows_free, 1)

            pe.wait_ge(w1_ready, 1)
            for b in range(GROUPS):
                pe.wait_ge(x1_ready, b + 1)
                pe.wait_ge(tr_copied, GROUPS + b - 1)
                transpose_group(x1, bank[4 + b % 2], b).then_inc(tr_done, 1)
                pe.wait_ge(tr_copied, GROUPS + b + 1)
                for k in range(4):
                    if b >= 1 and k % 2 == 0:
                        pe.wait_ge(feat_copied, 2 * b - 1 + k // 2)
                    last = nc.tensor.matmul(bank[6 + k // 2][:, k % 2 * 2 * FN:(k % 2 + 1) * 2 * FN], x1_tr[:, (4 * b + k) * P:(4 * b + k + 1) * P],
                                            w1_d[:, :, :].rearrange("p e n -> p (e n)"), start=True, stop=True)
                    if k % 2 == 1:
                        last.then_inc(feat_done, 1)
                nc.tensor.matmul(bank[b][0:2 * H, :], wsn[:, 0:2 * H], x1_tr[:, b * 512:(b + 1) * 512],
                                 start=True, stop=True).then_inc(srow_done, 1)

            pe.wait_ge(srow_copied, 4)
            with pe.Fori(0, PAIRS) as pr:
                pe.wait_ge(g_loaded, pr + 1)
                for k in range(STEPS):
                    e, jt, t = k // T, k % T, k // 2
                    pe.wait_ge(mask_ready, STEPS * pr + k + 1)
                    pe.sem_inc(pe_passed, 1)
                    m8 = mask[k % RING].bitcast(FP8)
                    for it in range(T):
                        c0 = it % PER_BANK * C3
                        if jt == 0 and it == 2 * PER_BANK:
                            pe.wait_ge(acc_free, 2 * pr + e + 1)
                            pe.sem_inc(pe_passed, 1)
                        last = nc.tensor.matmul(bank[SUM_BANKS[e][it // PER_BANK]][:, c0:c0 + C3], m8[:, it * P:(it + 1) * P],
                                                g[:, jt, e, :, :].rearrange("p q c -> p (q c)"),
                                                start=(jt == 0 and it % PER_BANK == 0), stop=(jt == T - 1), skip_group_check=True)
                    last.then_inc(mask_free, 1)
                    if k % 4 == 0:
                        pe.wait_ge(sd_free, HALF * pr + t // 2 + 1)
                        pe.sem_inc(pe_passed, 1)
                    for j in range(k % 2 * HALF, k % 2 * HALF + HALF):
                        last = nc.tensor.matmul(bank[4 + t // 2 % 2][:, t % 2 * C3:(t % 2 + 1) * C3].rearrange("p (m c) -> p m c", c=D + 1),
                                                adj8[:, j, t * P:(t + 1) * P].bitcast(FP8),
                                                g[:, j, :, :, D + 1:C].rearrange("p e q c -> p (e q) c"),
                                                start=(j == 0), stop=(j == T - 1))
                    if k % 4 == 3:
                        last.then_inc(sd_done, 1)

            def transpose_pair(src, n, k):
                pe.wait_ge(xt_copied, n)
                nc.tensor.transpose(bank[6][:, 0:P], src[:, 2 * k:2 * k + 2, :].rearrange("p a f -> p (a f)"),
                                    ident[:, :]).then_inc(xt_done, 1)

            def add_product(w, n, k):
                pe.wait_ge(xt_copied, n + 1)
                nc.tensor.matmul(bank[k // 4][:, k % 4 * P:(k % 4 + 1) * P], xt2[:, k % 2, :], w,
                                 start=False, stop=False, skip_group_check=True).then_inc(y_added, 1)

            def spmm_part(it, n, jt0, jt1, banks=SP_BANKS):
                ring = len(banks)
                if jt0 == 0 and it >= ring:
                    pe.wait_ge(sp_free, n + it - ring + 1)
                    pe.sem_inc(pe_passed, 1)
                for jt in range(jt0, jt1):
                    last = nc.tensor.matmul(bank[banks[it % ring]][:, 0:3 * F], adj8[:, jt, it * P:(it + 1) * P].bitcast(FP8),
                                            parts[:, jt, :, :].rearrange("p q f -> p (q f)"), start=(jt == 0), stop=(jt == T - 1))
                if jt1 == T:
                    last.then_inc(sp_done, 1)

            def spmm_first(p, late):
                pe.wait_ge(terms_ready, 2 * p + 1)
                pe.sem_inc(pe_passed, 1)
                for it in range(2):
                    spmm_part(it, T * p, 0, T - late)
                pe.wait_ge(terms_ready, 2 * p + 2)
                pe.sem_inc(pe_passed, 1)
                for it in range(2):
                    spmm_part(it, T * p, T - late, T)

            pe.wait_ge(w2_loaded, 32)
            for grp in range(GROUPS + 1):
                if grp < GROUPS:
                    pe.wait_ge(x2_ready, grp + 1)
                    if grp >= 2:
                        pe.wait_ge(xt_copied, grp - 1)
                    transpose_group(feat, bank[6 + grp % 2], grp).then_inc(xt_done, 1)
                if grp >= 1:
                    j = grp - 1
                    pe.wait_ge(xt_copied, j + 1)
                    for k in range(4):
                        last = nc.tensor.matmul(bank[j][:, k * P:(k + 1) * P], xt8[:, j % 2, k * P:(k + 1) * P], w2_d[:, 0, :],
                                                start=(k == 0), stop=False, skip_group_check=True)
                    last.then_inc(y_added, 1)

            def cheb_pass(p, w):
                for k in range(TP + 2):
                    if k == 0:
                        spmm_first(p, 8)
                    elif k < TP:
                        spmm_part(2 * k, T * p, 0, T)
                        spmm_part(2 * k + 1, T * p, 0, T)
                    if k >= 2:
                        add_product(w, TP * p + GROUPS + k - 2, k - 2)
                    if 1 <= k <= TP:
                        pe.wait_ge(new_ready, TP * p + k)
                        transpose_pair(t_new, TP * p + GROUPS + k - 1, k - 1)

            with pe.Fori(0, K - 2) as p:
                cheb_pass(p, w2_d[:, bass.ds(p + 1, 1), :].rearrange("p a n -> p (a n)"))
            cheb_pass(K - 2, w2_d[:, K - 1, :])
            spmm_first(K - 1, 8)
            for it in range(2, T):
                spmm_part(it, T * (K - 1), 0, T, L3_BANKS)

        @block.vector
        def _(dve):
            chain = Chain(dve, dve_did)
            all_stat, all_root = stat, root
            v = nc.vector
            for buf in (w0_d[:, :], w1_d[:, :, :], wsn[:, :]):
                chain(v.memset(buf, 0.0))
            chain(v.memset(epsc[:, :], EPS))
            chain(v.memset(coef[:, 0:1], 1.0))
            chain(v.memset(coef[:, 1:K], 2.0))
            chain.wait()
            dve.sem_inc(w_zeroed, 1)
            v.memset(zeros, 0.0).then_inc(zero_ready, 1)

            dve.wait_ge(w_loaded, 16 * 8)
            att_b = g_val[:, 0:4, :, :].rearrange("p t e c -> p (t e c)")
            for m in range(2):
                for e in range(2):
                    rows = slice(e * F, (e + 1) * F)
                    tmp = g_res[rows, 0:2, :, :].rearrange("p t e c -> p (t e c)")[:, 0:F]
                    chain.do(v.tensor_tensor(tmp, w1_d[rows, e, 0:F], att_b[rows, m * F:(m + 1) * F], ALU.mult))
                    chain.do(v.tensor_reduce(w1_d[rows, e, F + m * H:F + (m + 1) * H],
                                             tmp.rearrange("p (h d) -> p h d", d=D), AX_X, ALU.add))
                    if m == 0:
                        chain.do(v.tensor_copy(wsn[rows, e * H:(e + 1) * H], w1_d[rows, e, F:F + H]))
            dve.sem_inc(w1_ready, 1)

            for grp in range(GROUPS):
                dve.wait_ge(prod_done, grp + 1)
                v.tensor_copy(xw[:, 8 * grp:8 * grp + 8, :].rearrange("p a f -> p (a f)"), bank[6 + grp % 2][:, :]).then_inc(prod_copied, 1)
            dve.wait_ge(prod_copied, GROUPS)
            dve.wait_ge(prod_done, GROUPS + 4)

            def split(dst, val, res):
                chain.do(v.tensor_copy(dst[0], val))
                chain.do(v.tensor_tensor(res, val, dst[0], ALU.subtract))
                chain.do(v.tensor_copy(dst[1], res))
                chain.do(v.tensor_tensor(res, res, dst[1], ALU.subtract))
                return v.tensor_copy(dst[2], res)

            def cast_rows(j, r, n, first=False):
                dve.wait_ge(rows_free, j + 1)
                for c in range(2):
                    q = r % 2 * 2 + c
                    dve.wait_ge(stage_loaded[q], 16 * n)
                    v.tensor_scalar(row_buf[r][:, c * NH // 4:(c + 1) * NH // 4].bitcast(U8), stage[q], ONE_FP8, 0.0, ALU.mult, ALU.add,
                                    accum_out=deg2[:, c, bass.ds(j, 1)]).then_inc(stage_read_dve, 1)
                    if c == 0 and not first:
                        inverse_root(j - 1)
                dve.wait_ge(stage_read_dve, 2 * j + 2)
                v.tensor_tensor(deg[:, bass.ds(j, 1)], deg2[:, 0, bass.ds(j, 1)], deg2[:, 1, bass.ds(j, 1)], ALU.add).then_inc(deg_ready, 1)

            def inverse_root(j):
                dve.wait_ge(root_ready, j + 1)
                v.reciprocal(dinv[:, bass.ds(j, 1)], root[:, bass.ds(j, 1)]).then_inc(dinv_ready, 1)

            cast_rows(0, 0, 1, first=True)
            with dve.Fori(0, T // 4 - 1) as i:
                for r in range(1, 5):
                    cast_rows(4 * i + r, r % 4, 2 * i + r // 2 + 1)
            for r in range(1, 4):
                cast_rows(T - 4 + r, r, HALF - 2 + r // 2 + 1)
            inverse_root(T - 1)
            dve.wait_ge(dinv_ready, T)

            norms = [0]

            def layer_norm(dst, val, tmp, t0=0, t1=T):
                norms[0] += 1
                n, stat, root = norms[0], all_stat[:, t0:t1], all_root[:, t0:t1]
                chain.do(v.tensor_reduce(stat[:, :], val, AX_X, ALU.add))
                chain.do(v.tensor_scalar(stat[:, :], stat[:, :], 1.0 / F, None, ALU.mult))
                chain.do(v.tensor_tensor(val, val, bcast(stat[:, :], F), ALU.subtract))
                chain.do(v.tensor_tensor(tmp, val, val, ALU.mult))
                v.tensor_reduce(stat[:, :], tmp, AX_X, ALU.add).then_inc(var_ready, 1)
                dve.wait_ge(std_ready, n)
                chain.do(v.reciprocal(stat[:, :], root[:, :]))
                return v.tensor_tensor(dst, val, bcast(stat[:, :], F), ALU.mult)

            def centre(val, b):
                val, st = val[:, 8 * b:8 * b + 8, :], stat[:, 8 * b:8 * b + 8]
                chain.do(v.tensor_reduce(st, val, AX_X, ALU.add))
                chain.do(v.tensor_scalar(st, st, 1.0 / F, None, ALU.mult))
                v.tensor_tensor(val, val, bcast(st, F), ALU.subtract).then_inc(centred, 1)

            def square_sums(sq, b, n):
                dve.wait_ge(squared, n)
                v.tensor_reduce(stat[:, 8 * b:8 * b + 8], sq[:, 8 * b:8 * b + 8, :], AX_X, ALU.add).then_inc(var_ready, 1)
                norms[0] += 1

            def scale_rows(dst, val, b, n):
                st = stat[:, 8 * b:8 * b + 8]
                dve.wait_ge(std_ready, n)
                chain.do(v.reciprocal(st, root[:, 8 * b:8 * b + 8]))
                return v.tensor_tensor(dst[:, 8 * b:8 * b + 8, :], val[:, 8 * b:8 * b + 8, :], bcast(st, F), ALU.mult)

            dve.wait_ge(zb_ready, 1)
            for b in range(GROUPS + 2):
                if b < GROUPS:
                    t0, t1 = 8 * b, 8 * b + 8
                    dve.wait_ge(l0_evacuated, t1)
                    chain.do(v.tensor_tensor(work[:, t0:t1, :], work[:, t0:t1, :], xw[:, t0:t1, :], ALU.add))
                    chain.do(v.scalar_tensor_tensor(work[:, t0:t1, :], work[:, t0:t1, :], 0.0, feat[:, t0:t1, :], ALU.max, ALU.add))
                    centre(work, b)
                if 1 <= b <= GROUPS:
                    square_sums(xw, b - 1, b)
                if b == GROUPS:
                    scale_rows(x1, work, b - 1, b).then_inc(x1_ready, 1)
                if b >= 2:
                    for m in range(2 * b - 4, 2 * b - 2):
                        dve.wait_ge(feat_done, m + 1)
                        pr4 = bank[6 + m % 2][:, 0:4 * FN].rearrange("p (a n) -> p a n", a=4)
                        chain(v.tensor_copy(feat[:, 4 * m:4 * m + 4, :], pr4[:, :, 0:F]))
                        v.tensor_copy(fac[:, 0:2, 4 * m:4 * m + 4, :], pr4[:, :, F:FN].rearrange("p a (m h) -> p m a h", m=2)).then_inc(feat_copied, 1)
                if 1 <= b < GROUPS:
                    scale_rows(x1, work, b - 1, b).then_inc(x1_ready, 1)
            dve.wait_ge(feat_copied, 2 * GROUPS)
            chain.wait()
            s_f, n_f = fac[:, 0, :, :], fac[:, 1, :, :]
            chain(v.tensor_scalar(n_cols[:, 0, :, :].rearrange("p h t -> p t h"), n_f, -1.0, None, ALU.mult))
            chain(v.tensor_scalar(n_cols[:, 1, :, :].rearrange("p h t -> p t h"), n_f, STEP, None, ALU.mult))
            v.tensor_reduce(nmax[:, 0, :], n_f.rearrange("p t h -> p h t"), AX_X, ALU.max).then_inc(nmax_part, 1)
            dve.wait_ge(nmax_ready, 1)
            top = nmax[:, 1, :].unsqueeze(1).to_broadcast([P, T, H])
            chain(v.tensor_tensor(fac[:, 0, :, :], s_f, top, ALU.add))
            chain(v.tensor_tensor(fac[:, 1, :, :], n_f, top, ALU.subtract))
            chain.wait()
            chain(v.tensor_scalar(fac[:, 2, :, :], fac[:, 0, :, :], 0.0, -(1.0 - SLOPE), ALU.max, ALU.mult))
            chain(v.tensor_scalar(fac[:, 3, :, :], fac[:, 1, :, :], SLOPE, None, ALU.mult))
            chain.wait()
            v.tensor_scalar(fac[:, 0, :, :], fac[:, 0, :, :], 0.0, 1.0 - SLOPE, ALU.min, ALU.mult).then_inc(exp_in, 1)

            mine_of = [on_dve(k) for k in range(STEPS)]
            nd, na = sum(mine_of), STEPS - sum(mine_of)
            dve.wait_ge(srow_copied, 4)

            def evac_head(pr, e, part):
                for m in (2 * part, 2 * part + 1):
                    t0, t1 = m * PER_BANK, min(T, (m + 1) * PER_BANK)
                    ins = v.tensor_reduce(r_h[:, e, t0:t1, :], bank[SUM_BANKS[e][m]][:, 0:(t1 - t0) * C3].rearrange("p (t q c) -> p t c q", q=3, c=C), AX_X, ALU.add)
                    if m % 2 == 0 or part == 0:
                        chain(ins)
                if part == 1:
                    ins.then_inc(acc_free, 1)

            def evac_sd(pr, m):
                dve.wait_ge(sd_done, HALF * pr + m + 1)
                v.tensor_reduce(s_d[:, 2 * m:2 * m + 2, :, :].rearrange("p t e c -> p (t e) c"),
                                bank[4 + m % 2][:, 0:2 * C3].rearrange("p (t q c) -> p t c q", t=4, q=3), AX_X, ALU.add)\
                    .then_inc(sd_free, 1)

            def conj(pr, k):
                if mine_of[k]:
                    dve.wait_ge(cmp_dve, nd * pr + sum(mine_of[:k + 1]))
                else:
                    dve.wait_ge(cmp_act, na * pr + (k + 1 - sum(mine_of[:k + 1])))
                m32 = mask[k % RING].bitcast(I32)
                a32 = adj8[:, k % T, :].bitcast(I32)
                v.tensor_tensor(m32, m32, a32, ALU.bitwise_and).then_inc(mask_ready, 1)

            first = mine_of.index(True)

            def compare(pr, k):
                e = k // T
                if k % T == mine_of[e * T:].index(True):
                    dve.wait_ge(row_loaded[e], 16 * pr + 16)
                dve.wait_ge(mask_free, STEPS * pr + k + 1)
                v.tensor_scalar(mask[k % RING].bitcast(U8), s_row[e], n_cur[:, k:k + 1], ONE_FP8, ALU.is_gt, ALU.mult)\
                    .then_inc(cmp_dve, 1)

            def finish_tail(pr):
                evac_sd(pr, HALF - 1)
                evac_head(pr, 1, 0)
                chain.wait()
                dve.wait_ge(acc_free, 2 * pr + 3)
                dve.wait_ge(sd_free, HALF * pr + HALF + 2)
                dve.sem_inc(sums_ready, 1)

            def finish_head(pr, e):
                dve.wait_ge(sd_done, HALF * pr + HALF // 2 * (e + 1))
                evac_head(pr, e, 1)

            def begin(pr):
                v.tensor_copy(n_cur, n_cols[:, 0, bass.ds(2 * pr, 2), :].rearrange("p h t -> p (h t)")).then_inc(cols_ready, 1)
                dve.wait_ge(cols_ready, pr + 1)
                compare(pr, first)
                finish_head(pr - 1, 1)
                dve.wait_ge(g_made, pr)
                v.tensor_copy(aux[:, 0:T * C3].bitcast(BF16), aux[:, T * C3:2 * T * C3].bitcast(BF16)).then_inc(g_loaded, 1)

            def steps(pr, k0, k1):
                for k in range(k0, k1):
                    if k < STEPS and mine_of[k] and k != first:
                        compare(pr, k)
                    if k >= 1:
                        conj(pr, k - 1)
                    if k == 7:
                        dve.wait_ge(sums_used, pr + 1)
                    if k in (T, STEPS):
                        dve.wait_ge(cmp_dve, nd * pr + sum(mine_of[:k]))
                        dve.sem_inc(row_free[k // T - 1], 1)
                    if k >= 7 and k % 4 == 3:
                        evac_sd(pr, (k - 7) // 4)
                    if k == T + 1:
                        finish_head(pr, 0)
                        evac_head(pr, 0, 0)

            v.tensor_copy(n_cur, n_cols[:, 0, 0:2, :].rearrange("p h t -> p (h t)")).then_inc(cols_ready, 1)
            dve.wait_ge(exp_out, 1)
            prepare(v, chain, 0, g).then_inc(g_loaded, 1)
            dve.wait_ge(cols_ready, 1)
            compare(0, first)
            steps(0, 0, 2)
            with dve.Fori(0, PAIRS - 1) as pr:
                chain.body(pr, 2 * 3)
                steps(pr, 2, STEPS + 1)
                begin(pr + 1)
                steps(pr + 1, 0, 2)
                finish_tail(pr)
                chain.end(PAIRS - 1)
            steps(PAIRS - 1, 2, 8)
            v.reciprocal(den[:, :, 0:H - 2], den[:, :, 0:H - 2]).then_inc(den_inverted, 1)
            steps(PAIRS - 1, 8, STEPS + 1)
            finish_head(PAIRS - 1, 1)
            finish_tail(PAIRS - 1)

            dve.wait_ge(sums_used, PAIRS)
            combine(v, chain, PAIRS - 1)
            chain.do(v.reciprocal(den[:, :, H - 2:H], den[:, :, H - 2:H]))
            chain.do(divide(v, chain, H - 2, H))
            dve.wait_ge(divided, 1)

            dve.wait_ge(x1_back, 16)
            for b in range(GROUPS + 3):
                if b < GROUPS:
                    t0, t1 = 8 * b, 8 * b + 8
                    fg = feat[:, t0:t1, :]
                    chain.do(v.scalar_tensor_tensor(fg, fg, 0.0, x1_b[:, t0:t1, :], ALU.max, ALU.add))
                    centre(feat, b)
                if 1 <= b <= GROUPS:
                    square_sums(big2, b - 1, GROUPS + b)
                if 2 <= b <= GROUPS + 1:
                    t0, t1 = 8 * b - 16, 8 * b - 8
                    dve.wait_ge(part_cast[0], b - 1)
                    v.tensor_tensor(big2[:, t0:t1, :], feat[:, t0:t1, :], parts[:, t0:t1, 0, :], ALU.subtract).then_inc(rest_ready, 1)
                if 3 <= b:
                    t0, t1 = 8 * b - 24, 8 * b - 16
                    dve.wait_ge(part_cast[1], b - 2)
                    v.tensor_tensor(big2[:, t0:t1, :], big2[:, t0:t1, :], parts[:, t0:t1, 1, :], ALU.subtract).then_inc(rest2_ready, 1)
                if 1 <= b <= GROUPS:
                    scale_rows(feat, feat, b - 1, GROUPS + b).then_inc(x2_ready, 1)
            dve.wait_ge(part_cast[2], GROUPS)

            def all_parts(val, res, dst):
                return split([dst[:, :, q, :] for q in range(3)], val, res)

            res = aux[:, 0:4 * F].rearrange("p (a f) -> p a f", f=F)
            FLAT = 3 * F

            def new_pair(p, k, scale):
                for a in range(2):
                    dve.wait_ge(sp_done, T * p + 2 * k + a + 1)
                    v.tensor_reduce(res[:, a, :], bank[SP_BANKS[(2 * k + a) % 3]][:, 0:3 * F].rearrange("p (q f) -> p f q", q=3), AX_X, ALU.add)\
                        .then_inc(sp_free, 1)
                if k == 0:
                    dve.wait_ge(xt_done, TP * p + GROUPS)
                    dve.wait_ge(shifted, 2 * p + 1)
                dve.wait_ge(sp_free, T * p + 2 * k + 2)
                v.scalar_tensor_tensor(t_new[:, 2 * k:2 * k + 2, :], res[:, 0:2, :], scale, t_old[:, 2 * k:2 * k + 2, :],
                                       ALU.mult, ALU.subtract).then_inc(new_ready, 1)
                dve.wait_ge(new_ready, TP * p + k + 1)

            with dve.Fori(0, K - 2) as p:
                chain.body(p, TP * 5 + 1)
                for k in range(TP):
                    new_pair(p, k, coef[:, bass.ds(p, 1)])
                    dst = parts_new
                    if k == TP - 1:
                        dst = parts
                        chain.do(v.tensor_copy(parts[:, 0:T - 2, :, :], parts_new[:, 0:T - 2, :, :]))
                        dve.sem_inc(terms_ready, 1)
                    chain.do(split([dst[:, 2 * k:2 * k + 2, q, :] for q in range(3)], t_new[:, 2 * k:2 * k + 2, :], res[:, 2:4, :]))
                dve.sem_inc(terms_ready, 1)
                chain.end(K - 2)

            def x3_tiles(b, stages):
                t0, t1 = 8 * b, 8 * b + 8
                x3, tmp, st = feat[:, t0:t1, :], big2[:, 8:16, :], stat[:, t0:t1]
                dst = parts_new
                if t1 == T:
                    dst = parts
                hi, mid, lo = [dst[:, t0:t1, q, :] for q in range(3)]
                if 0 in stages:
                    dve.wait_ge(y_added, TP * (K - 2) + GROUPS + t1 // 2)
                    chain.do(v.tensor_tensor(x3, bank[b][:, :].rearrange("p (t f) -> p t f", f=F), x3, ALU.add))
                    chain.do(v.tensor_reduce(st, x3, AX_X, ALU.add))
                    chain.do(v.tensor_scalar(st, st, 1.0 / F, None, ALU.mult))
                    chain.do(v.tensor_tensor(x3, x3, bcast(st, F), ALU.subtract))
                if 1 in stages:
                    chain.do(v.tensor_tensor(tmp, x3, x3, ALU.mult))
                    v.tensor_reduce(st, tmp, AX_X, ALU.add).then_inc(var_ready, 1)
                    norms[0] += 1
                if 2 in stages:
                    dve.wait_ge(std_ready, 2 * GROUPS + b + 1)
                    chain.do(v.reciprocal(st, root[:, t0:t1]))
                    chain.do(v.tensor_tensor(x3, x3, bcast(st, F), ALU.mult))
                    chain.do(v.tensor_copy(hi, x3))
                    chain.do(v.tensor_tensor(tmp, x3, hi, ALU.subtract))
                if 3 in stages:
                    chain.do(v.tensor_copy(mid, tmp))
                    chain.do(v.tensor_tensor(tmp, tmp, mid, ALU.subtract))
                    chain.do(v.tensor_copy(lo, tmp))

            for k in range(TP):
                new_pair(K - 2, k, 2.0)
                if k >= 5:
                    b, stage_of_k = (k - 5) // 4, (k - 5) % 4
                    x3_tiles(b, [stage_of_k])
                    if k == TP - 1:
                        x3_tiles(b, [3])
            chain.do(v.tensor_copy(parts[:, 0:T - 8, :, :], parts_new[:, 0:T - 8, :, :]))
            dve.sem_inc(terms_ready, 1)
            x3_tiles(GROUPS - 1, range(4))
            dve.sem_inc(terms_ready, 1)

            for t0, t1 in L3_STEPS:
                x3, ax, y = feat[:, t0:t1, :], t_new[:, t0:t1, :], t_old[:, t0:t1, :]
                chain.do(v.tensor_scalar(y, x3, -0.1, 1.0, ALU.mult, ALU.add))
                chain.do(v.tensor_tensor(y, y, x3, ALU.add))
                for it in range(t0, t1):
                    dve.wait_ge(sp_done, T * (K - 1) + it + 1)
                    v.tensor_reduce(t_new[:, it, :], bank[L3_BANKS[it % 6]][:, 0:3 * F].rearrange("p (q f) -> p f q", q=3), AX_X, ALU.add)\
                        .then_inc(sp_free, 1)
                dve.wait_ge(sp_free, T * (K - 1) + t1)
                chain.do(v.scalar_tensor_tensor(ax, ax, 0.01, x3, ALU.mult, ALU.mult))
                chain.do(v.tensor_reduce(stat[:, t0:t1], ax, AX_X, ALU.add))
                chain.do(v.tensor_tensor(y, y, bcast(stat[:, t0:t1], F), ALU.subtract))
                layer_norm(x3, y, ax, t0, t1).then_inc(out_ready, 1)


_INS = ['x', 'adj', 'L0_gnn_W', 'L0_gnn_b', 'L1_gnn_W', 'L1_gnn_att_self', 'L1_gnn_att_neigh', 'L1_gnn_bias', 'L2_gnn_weight']


def kernel(**inputs):
    import numpy as _np
    import concourse.bacc as _bacc
    from concourse import mybir as _mybir
    from concourse.bass_utils import run_bass_kernel_spmd as _run

    nc = _bacc.Bacc("TRN2", target_bir_lowering=False, num_devices=1, dynamic_dma_scratch_size=1024)
    arrays, args = {}, []
    for name in _INS:
        a = _np.ascontiguousarray(inputs[name])
        arrays[f"in_{name}_dram"] = a
        args.append(nc.dram_tensor(f"in_{name}_dram", a.shape, _mybir.dt.from_np(a.dtype), kind="ExternalInput").ap())
    n, f = inputs["x"].shape
    args.append(nc.dram_tensor("out_0_dram", (n, f), _mybir.dt.float32, kind="ExternalOutput").ap())
    args.append(nc.dram_tensor("scratch_rows", (8, n), _mybir.dt.float32, kind="Internal").ap())
    args.append(nc.dram_tensor("scratch_x", (n, f), _mybir.dt.float32, kind="Internal").ap())
    graph_layers(nc, *args)
    r = _run(nc, [arrays], core_ids=[0])
    return r.results[0]["out_0_dram"]
```

```python
from contextlib import ExitStack

import concourse.bass as bass
from concourse import mybir

P = 128
F32, BF16 = mybir.dt.float32, mybir.dt.bfloat16
FP8, U8, I32 = mybir.dt.float8e4, mybir.dt.uint8, mybir.dt.int32
ALU = mybir.AluOpType
ACT = mybir.ActivationFunctionType
AX_X = mybir.AxisListType.X
RMAX = bass.bass_isa.ReduceOp.max

ONE_FP8 = 56.0
STEP = float(2.0 ** 60)
SLOPE = 0.2
EPS = 1e-5
RING = 5
DVE_SHARE = 26, 64


def on_dve(k):
    part, whole = DVE_SHARE
    return (k + 1) * part // whole > k * part // whole


class Chain:

    def __init__(self, eng, sem, passed=None):
        self.passed = passed
        self.eng, self.sem, self.n, self.loop = eng, sem, 0, 0

    def __call__(self, ins):
        ins.then_inc(self.sem, 1)
        self.n += 1

    def wait(self):
        self.eng.wait_ge(self.sem, self.loop + self.n)
        if self.passed is not None:
            self.eng.sem_inc(self.passed, 1)

    def do(self, ins):
        self(ins)
        self.wait()

    def body(self, i, per):
        self.start, self.per, self.loop = self.n, per, i * per

    def end(self, count):
        assert self.n - self.start == self.per, (self.n - self.start, self.per)
        self.n, self.loop = self.start + self.per * count, 0


def graph_layers(nc, x, adj, w0, b0, w1, att_self, att_neigh, bias1, w2, out, sc_rows, sc_x):
    N, F = x.shape
    H, D = att_self.shape
    K = w2.shape[0]
    T = N // P
    TP = T // 2
    PAIRS = H // 2
    C = 2 * (D + 1)
    C3 = 3 * C
    PER_BANK = 512 // C3
    FN = F + 2 * H
    STEPS = 2 * T
    assert (N, F, H * D, K) == (4096, 64, F, 4)

    x_t = x.rearrange("(t p) f -> p t f", p=P)
    out_t = out.rearrange("(t p) f -> p t f", p=P)
    sc_x_t = sc_x.rearrange("(p t) f -> p t f", p=P)
    adj_t = adj.rearrange("(t p) n -> t p n", p=P)

    with ExitStack() as ctx:
        def sb(name, shape, dt=F32):
            return ctx.enter_context(nc.sbuf_tensor(name, shape, dt))

        def sem(name):
            return ctx.enter_context(nc.semaphore(name))

        adj8 = sb("adj8", [P, T, N], U8)
        big = sb("big", [P, 3 * N])
        feat = sb("feat", [P, T, F])
        aux = sb("aux", [P, 2 * T * C3], F32)
        r_h = sb("r_h", [P, 2, T, C])
        s_d = sb("s_d", [P, T, 2, D + 1])
        den = sb("den", [P, T, H])
        fac = sb("fac", [P, 4, T, H])
        n_cols = sb("n_cols", [P, 2, H, T])
        cols = sb("cols", [P, 2, 2 * T])
        n_cur, k_cur = cols[:, 0, :], cols[:, 1, :]
        g_val = sb("g_val", [P, T, 2, C])
        mask_4 = sb("mask_4", [P, N // 4])
        ident = sb("ident", [P, P])
        b0_b = sb("b0_b", [P, F])
        b1_b = sb("b1_b", [P, F])
        deg2 = sb("deg2", [P, 2, T])
        deg = sb("deg", [P, T])
        dinv = sb("dinv", [P, T])
        root = sb("root", [P, T])
        stat = sb("stat", [P, T])
        nmax = sb("nmax", [P, 2, H])
        epsc = sb("epsc", [P, 1])

        bank = [ctx.enter_context(nc.psum_tensor(f"bank{b}", [P, 512], F32)) for b in range(8)]

        NH = N // 2
        stage = [big[:, NH * q:NH * (q + 1)] for q in range(4)]
        row_buf = [big[:, 2 * N + N // 4 * r:2 * N + N // 4 * (r + 1)] for r in range(4)]
        zeros = row_buf[0].bitcast(BF16)[:, 0:512]
        x_tr = adj8[:, T - 4:T, :].rearrange("p a n -> p (a n)").bitcast(F32)[:, 0:TP * P]
        xw = aux[:, 0:T * F].rearrange("p (t f) -> p t f", f=F)
        z_res = aux[:, T * F:T * F + 2 * F].rearrange("p (a f) -> p a f", f=F)
        z_part = aux[:, T * F + 2 * F:T * F + 5 * F].bitcast(BF16).rearrange("p (u q f) -> p u q f", u=2, q=3)
        x1 = big[:, N:N + T * F].rearrange("p (t f) -> p t f", f=F)
        work = big[:, 0:T * F].rearrange("p (t f) -> p t f", f=F)
        x1_b = work
        x1_tr = big[:, 2 * N:2 * N + TP * P]
        s_rows = big[0:8 * H, 2 * N + TP * P:2 * N + TP * P + T // 8 * P].rearrange("p (b c) -> p b c", c=P)
        s_row = [big[:, 0:N], big[:, N:2 * N]]
        mask = [big[:, 2 * N + N // 4 * r:2 * N + N // 4 * (r + 1)] for r in range(4)] + [mask_4[:, :]]
        g = aux[:, 0:T * C3].bitcast(BF16).rearrange("p (t e q c) -> p t e q c", t=T, e=2, q=3)
        g_next = aux[:, T * C3:2 * T * C3].bitcast(BF16).rearrange("p (t e q c) -> p t e q c", t=T, e=2, q=3)
        TF = T * F

        early = r_h[:, :, :, :].rearrange("p e t c -> p (e t c)")
        w0_d = early[:, 0:2 * F]
        w1_d = early[:, 2 * F:2 * F + 2 * FN].rearrange("p (e n) -> p e n", e=2)
        w2_d = aux[:, T * F + 8:T * F + 8 + K * 2 * F].rearrange("p (k o) -> p k o", k=K)
        xt8 = g_val[:, :, :, :].rearrange("p t e c -> p (t e c)")[:, 0:8 * P].rearrange("p (a c) -> p a c", a=2)
        acc = big[:, 0:3 * TF].rearrange("p (m t f) -> p m t f", m=K - 1, f=F)
        parts_of = big[:, 3 * TF:6 * TF].bitcast(BF16).rearrange("p (w t q f) -> p w t q f", w=2, q=3, f=F)
        parts = parts_of[:, 0]
        b_3 = big[:, 3 * TF + 3 * TF // 2:3 * TF + 3 * TF // 2 + TF].rearrange("p (t f) -> p t f", f=F)
        scratch = aux[:, 0:T * F].rearrange("p (t f) -> p t f", f=F)

        x_loaded = [sem("x0_loaded"), sem("x1_loaded")]
        w_loaded = sem("w_loaded")
        w_zeroed = sem("w_zeroed")
        w_issued = sem("w_issued")
        stage_loaded = [sem(f"stage{q}_loaded") for q in range(4)]
        deg_ready = sem("deg_ready")
        stage_read_act = sem("stage_read_act")
        stage_read_dve = sem("stage_read_dve")
        const_ready = sem("const_ready")
        dve_did = sem("dve_did")
        act_passed = sem("act_passed")
        pe_passed = sem("pe_passed")
        pool_passed = sem("pool_passed")
        dve_passed = sem("dve_passed")
        act_did = sem("act_did")
        pool_did = sem("pool_did")
        tr_done = sem("tr_done")
        tr_copied = sem("tr_copied")
        prod_done = sem("prod_done")
        prod_copied = sem("prod_copied")
        zero_ready = sem("zero_ready")
        dinv_ready = sem("dinv_ready")
        root_ready = sem("root_ready")
        z_ready = sem("z_ready")
        zb_ready = sem("zb_ready")
        rows_free = sem("rows_free")
        x1_ready = sem("x1_ready")
        bank_summed = sem("bank_summed")
        l0_evacuated = sem("l0_evacuated")
        centred = sem("centred")
        squared = sem("squared")
        var_ready = sem("var_ready")
        std_ready = sem("std_ready")
        w1_ready = sem("w1_ready")
        feat_done = sem("feat_done")
        feat_copied = sem("feat_copied")
        srow_done = sem("srow_done")
        srow_copied = sem("srow_copied")
        srow_stored = sem("srow_stored")
        x1_stored = sem("x1_stored")
        nmax_part = sem("nmax_part")
        nmax_ready = sem("nmax_ready")
        exp_in = sem("exp_in")
        exp_out = sem("exp_out")
        cols_ready = sem("cols_ready")
        row_loaded = [sem("row0_loaded"), sem("row1_loaded")]
        row_free = [sem("row0_free"), sem("row1_free")]
        cmp_act = sem("cmp_act")
        cmp_dve = sem("cmp_dve")
        mask_ready = sem("mask_ready")
        mask_free = sem("mask_free")
        acc_free = sem("acc_free")
        sd_done = sem("sd_done")
        sd_free = sem("sd_free")
        g_made = sem("g_made")
        g_loaded = sem("g_loaded")
        sums_ready = sem("sums_ready")
        sums_used = sem("sums_used")
        x1_back = sem("x1_back")
        den_inverted = sem("den_inverted")
        divided = sem("divided")
        w2_zeroed = sem("w2_zeroed")
        w2_loaded = sem("w2_loaded")
        rhs_ready = sem("rhs_ready")
        x2_ready = sem("x2_ready")
        rest_ready = sem("rest_ready")
        rest2_ready = sem("rest2_ready")
        part_cast = [sem(f"part{q}_cast") for q in range(3)]
        b3_done = sem("b3_done")
        b3_copied = sem("b3_copied")
        u_done = sem("u_done")
        u_copied = sem("u_copied")
        sp_done = sem("sp_done")
        sp_free = sem("sp_free")
        xt_done = sem("xt_done")
        xt_copied = sem("xt_copied")
        out_ready = sem("out_ready")
        out_stored = sem("out_stored")
        block = ctx.enter_context(nc.Block())

        SUM_BANKS = (2, 3, 0, 1), (6, 7, 0, 1)
        SP_BANKS = 4, 5, 6, 7, 0, 1
        RHS_ENDS = T // 2, T - 8, T
        HALF = T // 2
        GROUPS = T // 8
        L3_STEPS = [(t, t + 4) for t in range(0, T - 4, 4)] + [(T - 4, T - 2), (T - 2, T)]

        def bcast(ap2, n):
            return ap2.unsqueeze(2).to_broadcast([P, ap2.shape[1], n])

        def row_of(pr, e):
            return 16 * pr + (64 if e == 0 else 16)

        def buffer_free(pr, k):
            user = k - RING
            if user < 0:
                user = k + (STEPS - 1 - k) // RING * RING - STEPS
            return STEPS * pr + user + 1 + RING

        def prepare(eng, chain, pr, dst):
            fh = feat[:, :, bass.ds(pr * 2 * D, 2 * D)].rearrange("p t (e d) -> p t e d", e=2)
            for m, o in ((1, 0), (3, D + 1)):
                fm = fac[:, m, :, bass.ds(pr * 2, 2)]
                chain(eng.tensor_tensor(g_val[:, :, :, o:o + D], fh, fm.unsqueeze(3).to_broadcast([P, T, 2, D]), ALU.mult))
                chain(eng.tensor_copy(g_val[:, :, :, o + D], fm))
            chain.wait()
            chain.do(eng.tensor_copy(dst[:, :, :, 0, :], g_val[:, :, :, :]))
            chain.do(eng.tensor_tensor(g_val[:, :, :, :], g_val[:, :, :, :], dst[:, :, :, 0, :], ALU.subtract))
            chain.do(eng.tensor_copy(dst[:, :, :, 1, :], g_val[:, :, :, :]))
            chain.do(eng.tensor_tensor(g_val[:, :, :, :], g_val[:, :, :, :], dst[:, :, :, 1, :], ALU.subtract))
            return eng.tensor_copy(dst[:, :, :, 2, :], g_val[:, :, :, :])

        def combine(eng, chain, pr):
            a = fac[:, 0, :, bass.ds(pr * 2, 2)]
            c = fac[:, 2, :, bass.ds(pr * 2, 2)]
            for e in range(2):
                mb, md = r_h[:, e, :, 0:D + 1], r_h[:, e, :, D + 1:C]
                chain(eng.tensor_tensor(md, s_d[:, :, e, :], md, ALU.subtract))
                chain(eng.tensor_tensor(mb, mb, bcast(a[:, :, e], D + 1), ALU.mult))
            chain.wait()
            for e in range(2):
                md = r_h[:, e, :, D + 1:C]
                chain(eng.tensor_tensor(md, md, bcast(c[:, :, e], D + 1), ALU.mult))
            chain.wait()
            for e in range(2):
                mb, md = r_h[:, e, :, 0:D + 1], r_h[:, e, :, D + 1:C]
                chain(eng.tensor_tensor(feat[:, :, bass.ds((pr * 2 + e) * D, D)], mb[:, :, 0:D], md[:, :, 0:D], ALU.add))
                chain(eng.tensor_tensor(den[:, :, bass.ds(pr * 2 + e, 1)], mb[:, :, D:D + 1], md[:, :, D:D + 1], ALU.add))
            chain.wait()

        def divide(eng, chain, h0, h1):
            f = feat[:, :, h0 * D:h1 * D]
            f4 = f.rearrange("p t (h d) -> p t h d", d=D)
            chain.do(eng.tensor_tensor(f4, f4, den[:, :, h0:h1].unsqueeze(3).to_broadcast([P, T, h1 - h0, D]), ALU.mult))
            return eng.tensor_tensor(f, f, b1_b[:, h0 * D:h1 * D].unsqueeze(1).to_broadcast([P, T, (h1 - h0) * D]), ALU.add)

        @block.sync
        def _(sp):
            for m in range(2):
                sp.dma_start(feat[:, HALF * m:HALF * (m + 1), :], x_t[:, HALF * m:HALF * (m + 1), :]).then_inc(x_loaded[m], 16)
            sp.wait_ge(w_issued, 1)
            for q in range(4):
                sp.dma_start(stage[q], adj_t[q // 2][:, q % 2 * NH:(q % 2 + 1) * NH]).then_inc(stage_loaded[q], 16)
            with sp.Fori(1, HALF) as i:
                for q in range(4):
                    sp.wait_ge(stage_read_act, 4 * i + q - 3)
                    sp.wait_ge(stage_read_dve, 4 * i + q - 3)
                    sp.dma_start(stage[q], adj_t[bass.ds(2 * i + q // 2, 1), :, q % 2 * NH:(q % 2 + 1) * NH].rearrange("a p n -> (a p) n"))\
                        .then_inc(stage_loaded[q], 16)

            def store_x1(b):
                sp.wait_ge(x1_ready, b + 1)
                sp.dma_start(sc_x_t[:, 8 * b:8 * b + 8, :], x1[:, 8 * b:8 * b + 8, :]).then_inc(x1_stored, 16)

            s_of_head = sc_rows.rearrange("(t h) c -> h t c", h=H)
            row_of_tiles = [row.rearrange("p (t c) -> p t c", c=P) for row in s_row]

            def store_s(b):
                sp.wait_ge(srow_copied, b + 1)
                sp.dma_start(sc_rows[8 * H * b:8 * H * (b + 1), :], s_rows[:, b, :]).then_inc(srow_stored, 16)

            def load_s(b):
                sp.dma_start(row_of_tiles[0][:, 8 * b:8 * b + 8, :], s_of_head[0:1, 8 * b:8 * b + 8, :].to_broadcast([P, 8, P]))\
                    .then_inc(row_loaded[0], 16)

            store_x1(0)
            store_s(0)
            sp.wait_ge(srow_stored, 16)
            sp.wait_ge(x1_ready, 2)
            load_s(0)
            store_x1(1)
            store_s(1)
            store_x1(2)
            store_s(2)
            sp.wait_ge(srow_stored, 48)
            load_s(2)
            sp.wait_ge(x1_ready, 4)
            store_s(3)
            load_s(1)
            sp.wait_ge(srow_stored, 64)
            load_s(3)
            store_x1(3)
            sp.wait_ge(x1_stored, 64)
            sp.wait_ge(tr_done, 2 * GROUPS)
            sp.dma_start(row_of_tiles[1], s_of_head[1:2, :, :].to_broadcast([P, T, P])).then_inc(row_loaded[1], 16)
            with sp.Fori(1, PAIRS) as pr:
                for e in range(2):
                    sp.wait_ge(row_free[e], 2 * pr)
                    sp.dma_start(row_of_tiles[e], s_of_head[bass.ds(2 * pr + e, 1), :, :].to_broadcast([P, T, P])).then_inc(row_loaded[e], 16)
            sp.wait_ge(row_free[0], 2 * PAIRS)
            sp.dma_start(x1_b, sc_x_t).then_inc(x1_back, 16)
            sp.wait_ge(w2_zeroed, 1)
            for m in range(K):
                for e in range(2):
                    sp.dma_start(w2_d[e * F:(e + 1) * F, m, e * F:(e + 1) * F], w2[K - 1 - m]).then_inc(w2_loaded, 16)
            for m, (t0, t1) in enumerate(L3_STEPS):
                sp.wait_ge(out_ready, m + 1)
                sp.dma_start(out_t[:, t0:t1, :], feat[:, t0:t1, :]).then_inc(out_stored, 16)
            sp.wait_ge(out_stored, 16 * len(L3_STEPS))

        @block.gpsimd
        def _(pool):
            chain = Chain(pool, pool_did, pool_passed)
            pool.sem_inc(sums_used, 1)
            chain.do(nc.gpsimd.memset(ident[:, :], 0.0))
            nc.gpsimd.affine_select(out=ident[:, :], in_=ident[:, :], compare_op=ALU.not_equal, fill=1.0,
                                    base=0, pattern=[[-1, P]], channel_multiplier=1).then_inc(const_ready, 1)
            pool.wait_ge(prod_copied, GROUPS)
            with pool.Fori(0, HALF) as i:
                chain.body(i, 2 * 7)
                for u in range(2):
                    t = bass.ds(2 * i + u, 1)
                    pool.wait_ge(rows_free, 2 * i + u + 3)
                    pool.wait_ge(dinv_ready, 2 * i + u + 1)
                    pool.sem_inc(pool_passed, 1)
                    chain.do(nc.gpsimd.tensor_tensor(xw[:, t, :], xw[:, t, :], dinv[:, t].unsqueeze(2).to_broadcast([P, 1, F]), ALU.mult))
                    chain.do(nc.gpsimd.tensor_copy(z_part[:, u, 0:1, :], xw[:, t, :]))
                    chain.do(nc.gpsimd.tensor_tensor(z_res[:, 0:1, :], xw[:, t, :], z_part[:, u, 0:1, :], ALU.subtract))
                    chain.do(nc.gpsimd.tensor_copy(z_part[:, u, 1:2, :], z_res[:, 0:1, :]))
                    chain.do(nc.gpsimd.tensor_tensor(z_res[:, 1:2, :], z_res[:, 0:1, :], z_part[:, u, 1:2, :], ALU.subtract))
                    nc.gpsimd.tensor_copy(z_part[:, u, 2:3, :], z_res[:, 1:2, :]).then_inc(z_ready, 1)
                    chain.do(nc.gpsimd.tensor_tensor(xw[:, t, :], xw[:, t, :], dinv[:, t].unsqueeze(2).to_broadcast([P, 1, F]), ALU.mult))
                    chain.do(nc.gpsimd.tensor_tensor(xw[:, t, :], xw[:, t, :], b0_b[:, :].unsqueeze(1), ALU.add))
                chain.end(HALF)
            pool.sem_inc(zb_ready, 1)
            pool.wait_ge(nmax_part, 1)
            nc.gpsimd.partition_all_reduce(nmax[:, 1, :], nmax[:, 0, :], P, RMAX).then_inc(nmax_ready, 1)

            pool.wait_ge(exp_out, 2)
            with pool.Fori(0, PAIRS - 1) as pr:
                chain.body(pr, 8 + 10)
                pool.wait_ge(g_loaded, pr + 1)
                prepare(nc.gpsimd, chain, pr + 1, g_next).then_inc(g_made, 1)
                pool.wait_ge(sums_ready, pr + 1)
                combine(nc.gpsimd, chain, pr)
                pool.sem_inc(sums_used, 1)
                chain.end(PAIRS - 1)
            pool.wait_ge(g_loaded, PAIRS)
            nc.gpsimd.memset(w2_d, 0.0).then_inc(w2_zeroed, 1)
            pool.wait_ge(den_inverted, 1)
            divide(nc.gpsimd, chain, 0, H - 2).then_inc(divided, 1)

        @block.scalar
        def _(act):
            chain = Chain(act, act_did, act_passed)
            act.wait_ge(w_zeroed, 1)
            for e in range(2):
                rows = slice(e * F, (e + 1) * F)
                act.dma_start(w0_d[rows, e * F:(e + 1) * F], w0).then_inc(w_loaded, 16)
                act.dma_start(w1_d[rows, e, 0:F], w1).then_inc(w_loaded, 16)
            act.dma_start(b0_b[:, :], b0.rearrange("(a n) -> a n", a=1).to_broadcast([P, F])).then_inc(w_loaded, 16)
            act.dma_start(b1_b[:, :], bias1.rearrange("h d -> (h d)").rearrange("(a n) -> a n", a=1).to_broadcast([P, F])).then_inc(w_loaded, 16)
            for m, att in enumerate((att_self, att_neigh)):
                act.dma_start(g_val[:, 0:4, :, :].rearrange("p t e c -> p (t e c)")[:, m * F:(m + 1) * F],
                              att.rearrange("h d -> (h d)").rearrange("(a n) -> a n", a=1).to_broadcast([P, F])).then_inc(w_loaded, 16)

            act.sem_inc(w_issued, 1)
            chain.do(nc.scalar.activation(root[:, 0:1], epsc[:, 0:1], ACT.Sqrt))

            def copy_transposed(dst, g, n):
                act.wait_ge(tr_done, n)
                nc.scalar.activation(dst[:, 4 * g * P:4 * (g + 1) * P], bank[4 + g % 2][:, :], ACT.Copy).then_inc(tr_copied, 1)

            for grp in range(GROUPS):
                copy_transposed(x_tr, grp, grp + 1)
            act.wait_ge(prod_done, GROUPS)

            def rows8(j, u, n):
                for c in range(2):
                    act.wait_ge(stage_loaded[2 * u + c], 16 * n)
                    nc.scalar.activation(adj8[:, bass.ds(j, 1), c * NH:(c + 1) * NH].rearrange("p a n -> p (a n)"), stage[2 * u + c],
                                         ACT.Copy, scale=ONE_FP8).then_inc(stage_read_act, 1)
                act.wait_ge(deg_ready, j + 1)
                nc.scalar.activation(root[:, bass.ds(j, 1)], deg[:, bass.ds(j, 1)], ACT.Sqrt, bias=1.0, scale=1.0 / ONE_FP8).then_inc(root_ready, 1)

            with act.Fori(0, HALF) as i:
                for u in range(2):
                    rows8(2 * i + u, u, i + 1)

            def norm_root(n, t0, t1):
                act.wait_ge(var_ready, n)
                nc.scalar.activation(root[:, t0:t1], stat[:, t0:t1], ACT.Sqrt, bias=epsc[:, 0:1], scale=1.0 / F).then_inc(std_ready, 1)

            def square(src, dst, n, b):
                act.wait_ge(centred, n)
                nc.scalar.activation(dst[:, 8 * b:8 * b + 8, :], src[:, 8 * b:8 * b + 8, :], ACT.Square).then_inc(squared, 1)

            def evacuate(b):
                for t in range(8 * b, 8 * b + 8):
                    nc.scalar.activation(work[:, t, :], bank[b][:, t % 8 * F:(t % 8 + 1) * F], ACT.Copy, scale=dinv[:, t:t + 1])\
                        .then_inc(l0_evacuated, 1)

            act.wait_ge(stage_read_dve, 2 * T)
            act.wait_ge(dinv_ready, T)
            for b in range(GROUPS + 2):
                if b + 1 < GROUPS:
                    if b + 1 < GROUPS - 1:
                        act.wait_ge(bank_summed, (GROUPS - 1) * (T - 1) + b + 2)
                    else:
                        act.wait_ge(rows_free, T + 4)
                    evacuate(b + 1)
                if b < GROUPS:
                    square(work, xw, b + 1, b)
                if 1 <= b <= GROUPS:
                    norm_root(b, 8 * b - 8, 8 * b)
                    copy_transposed(x1_tr, b - 1, GROUPS + b)
                if 2 <= b:
                    act.wait_ge(srow_done, b - 1)
                    nc.scalar.activation(s_rows[:, b - 2, :], bank[b - 2][0:8 * H, 0:P], ACT.Copy).then_inc(srow_copied, 1)
            for m in range(2):
                act.wait_ge(exp_in, m + 1)
                f = fac[:, :, :, :].rearrange("p (a m) t h -> p m a (t h)", m=2)[:, 1 - m, :, :]
                nc.scalar.activation(f, f, ACT.Exp).then_inc(exp_out, 1)
            chain.do(nc.scalar.activation(root[:, 0:1], epsc[:, 0:1], ACT.Sigmoid))

            na = sum(not on_dve(k) for k in range(STEPS))
            with act.Fori(0, PAIRS) as pr:
                chain.body(pr, 1)
                chain.do(nc.scalar.activation(k_cur, n_cols[:, 1, bass.ds(2 * pr, 2), :].rearrange("p h t -> p (h t)"), ACT.Copy))
                chain.end(PAIRS)
                for e in range(2):
                    act.wait_ge(row_loaded[e], row_of(pr, e))
                    mine = [k for k in range(e * T, (e + 1) * T) if not on_dve(k)]
                    for k in mine:
                        act.wait_ge(mask_free, buffer_free(pr, k))
                        act.sem_inc(act_passed, 1)
                        nc.scalar.activation(mask[k % RING].bitcast(FP8), s_row[e], ACT.Sigmoid,
                                             bias=k_cur[:, k:k + 1], scale=STEP, saturate=False).then_inc(cmp_act, 1)
                    act.wait_ge(cmp_act, na * pr + sum(not on_dve(k) for k in range((e + 1) * T)))
                    act.sem_inc(row_free[e], 1)

            def copy_xt8(j):
                act.wait_ge(xt_done, j + 1)
                nc.scalar.activation(xt8[:, j % 2, :], bank[6][:, :], ACT.Copy).then_inc(xt_copied, 1)

            def copy_b3(j):
                act.wait_ge(b3_done, j + 1)
                nc.scalar.activation(b_3[:, 8 * j:8 * j + 8, :], bank[7][:, :].rearrange("p (t f) -> p t f", f=F), ACT.Copy)\
                    .then_inc(b3_copied, 1)

            def copy_u(j):
                for k in range(4 * j, 4 * j + 4):
                    act.wait_ge(u_done, k + 1)
                    nc.scalar.activation(acc[:, :, 2 * k:2 * k + 2, :].rearrange("p m a f -> p m (a f)"),
                                         bank[k % 4][:, 0:3 * P].rearrange("p (m c) -> p m c", m=3), ACT.Copy).then_inc(u_copied, 1)

            def cast_part(q, b, src, ready, n):
                act.wait_ge(ready, n)
                nc.scalar.activation(parts[:, 8 * b:8 * b + 8, q, :], src[:, 8 * b:8 * b + 8, :], ACT.Copy).then_inc(part_cast[q], 1)

            chain.do(nc.scalar.activation(root[:, 0:1], epsc[:, 0:1], ACT.Sqrt))

            for b in range(GROUPS + 4):
                if 2 <= b < GROUPS + 2:
                    copy_xt8(b - 2)
                if b < GROUPS:
                    square(feat, scratch, GROUPS + b + 1, b)
                if 2 <= b < GROUPS + 2:
                    copy_b3(b - 2)
                if 1 <= b <= GROUPS:
                    norm_root(GROUPS + b, 8 * b - 8, 8 * b)
                if 2 <= b < GROUPS + 2:
                    cast_part(0, b - 2, b_3, b3_copied, b - 1)
                if 3 <= b < GROUPS + 3:
                    cast_part(1, b - 3, scratch, rest_ready, b - 2)
                if 4 <= b:
                    cast_part(2, b - 4, scratch, rest2_ready, b - 3)
                if b in (GROUPS + 1, GROUPS + 2):
                    act.wait_ge(part_cast[2], b - 3)
                    act.sem_inc(rhs_ready, 1)
                if 3 <= b < GROUPS + 2:
                    copy_u(b - 3)
            for q in range(3):
                act.wait_ge(part_cast[q], GROUPS)
            act.sem_inc(rhs_ready, 1)
            copy_u(GROUPS - 1)
            for b in range(GROUPS - 1):
                norm_root(2 * GROUPS + b + 1, 8 * b, 8 * b + 8)
            norm_root(3 * GROUPS, T - 8, T)
            for m, (t0, t1) in enumerate(L3_STEPS):
                norm_root(3 * GROUPS + m + 1, t0, t1)

        @block.tensor
        def _(pe):
            pe.sem_inc(rows_free, 4)
            pe.sem_inc(mask_free, RING)
            pe.sem_inc(acc_free, 1)
            pe.sem_inc(sd_free, 2)
            pe.sem_inc(sp_free, T % len(SP_BANKS))

            def transpose_group(src, dst, g):
                for k in range(4):
                    t = 8 * g + 2 * k
                    last = nc.tensor.transpose(dst[:, k * P:(k + 1) * P], src[:, t:t + 2, :].rearrange("p a f -> p (a f)"), ident[:, :])
                return last

            pe.wait_ge(const_ready, 1)
            for grp in range(GROUPS + 1):
                if grp < GROUPS:
                    if grp % (GROUPS // 2) == 0:
                        pe.wait_ge(x_loaded[grp // (GROUPS // 2)], 16)
                    if grp >= 2:
                        pe.wait_ge(tr_copied, grp - 1)
                    transpose_group(feat, bank[4 + grp % 2], grp).then_inc(tr_done, 1)
                if grp >= 1:
                    j = grp - 1
                    if j == 0:
                        pe.wait_ge(w_loaded, 16 * 8)
                    if j >= 2:
                        pe.wait_ge(prod_copied, j - 1)
                    pe.wait_ge(tr_copied, j + 1)
                    for k in range(4):
                        last = nc.tensor.matmul(bank[6 + j % 2][:, k * P:(k + 1) * P], x_tr[:, (4 * j + k) * P:(4 * j + k + 1) * P], w0_d[:, :],
                                                start=True, stop=True)
                    last.then_inc(prod_done, 1)

            pe.wait_ge(zero_ready, 1)
            for b in range(4):
                nc.tensor.matmul(bank[b][:, :], zeros[:, 0:P], zeros, start=True, stop=False, skip_group_check=True)\
                    .then_inc(prod_done, 1)
            with pe.Fori(0, T // 4) as i:
                for u in range(4):
                    pe.wait_ge(z_ready, 4 * i + u + 1)
                    pe.sem_inc(pe_passed, 1)
                    for it in range(T):
                        for q in range(3):
                            last = nc.tensor.matmul(bank[it // 8][:, (it % 8) * F:(it % 8 + 1) * F],
                                                    row_buf[u].bitcast(FP8)[:, it * P:(it + 1) * P], z_part[:, u % 2, q, :],
                                                    start=False, stop=False, skip_group_check=True)
                        if it % 8 == 7 and it < T - 1:
                            last.then_inc(bank_summed, 1)
                    last.then_inc(rows_free, 1)

            def transpose_s(b):
                pe.wait_ge(feat_copied, 2 * b + 2)
                nc.tensor.transpose(bank[b][0:8 * H, 0:P], fac[:, 0, 8 * b:8 * b + 8, :].rearrange("p t h -> p (t h)"), ident[:, :])\
                    .then_inc(srow_done, 1)

            pe.wait_ge(w1_ready, 1)
            for b in range(GROUPS):
                pe.wait_ge(x1_ready, b + 1)
                pe.wait_ge(tr_copied, GROUPS + b - 1)
                transpose_group(x1, bank[4 + b % 2], b).then_inc(tr_done, 1)
                if b >= 1:
                    transpose_s(b - 1)
                pe.wait_ge(tr_copied, GROUPS + b + 1)
                for k in range(4):
                    if b >= 1 and k % 2 == 0:
                        pe.wait_ge(feat_copied, 2 * b - 1 + k // 2)
                    last = nc.tensor.matmul(bank[6 + k // 2][:, k % 2 * 2 * FN:(k % 2 + 1) * 2 * FN], x1_tr[:, (4 * b + k) * P:(4 * b + k + 1) * P],
                                            w1_d[:, :, :].rearrange("p e n -> p (e n)"), start=True, stop=True)
                    if k % 2 == 1:
                        last.then_inc(feat_done, 1)
            transpose_s(GROUPS - 1)

            pe.wait_ge(srow_copied, 4)
            with pe.Fori(0, PAIRS) as pr:
                pe.wait_ge(g_loaded, pr + 1)
                for k in range(STEPS):
                    e, jt, t = k // T, k % T, k // 2
                    pe.wait_ge(mask_ready, STEPS * pr + k + 1)
                    pe.sem_inc(pe_passed, 1)
                    m8 = mask[k % RING].bitcast(FP8)
                    for it in range(T):
                        c0 = it % PER_BANK * C3
                        if jt == 0 and it == 2 * PER_BANK:
                            pe.wait_ge(acc_free, 2 * pr + e + 1)
                            pe.sem_inc(pe_passed, 1)
                        last = nc.tensor.matmul(bank[SUM_BANKS[e][it // PER_BANK]][:, c0:c0 + C3], m8[:, it * P:(it + 1) * P],
                                                g[:, jt, e, :, :].rearrange("p q c -> p (q c)"),
                                                start=(jt == 0 and it % PER_BANK == 0), stop=(jt == T - 1), skip_group_check=True)
                    last.then_inc(mask_free, 1)
                    if k % 4 == 0:
                        pe.wait_ge(sd_free, HALF * pr + t // 2 + 1)
                        pe.sem_inc(pe_passed, 1)
                    for j in range(k % 2 * HALF, k % 2 * HALF + HALF):
                        last = nc.tensor.matmul(bank[4 + t // 2 % 2][:, t % 2 * C3:(t % 2 + 1) * C3].rearrange("p (m c) -> p m c", c=D + 1),
                                                adj8[:, j, t * P:(t + 1) * P].bitcast(FP8),
                                                g[:, j, :, :, D + 1:C].rearrange("p e q c -> p (e q) c"),
                                                start=(j == 0), stop=(j == T - 1))
                    if k % 4 == 3:
                        last.then_inc(sd_done, 1)

            def spmm_part(it, n, w, jt0, jt1):
                ring = len(SP_BANKS)
                if jt0 == 0 and (it < T % ring or it >= ring):
                    pe.wait_ge(sp_free, n + it + (1 if it < ring else T % ring + 1 - ring))
                    pe.sem_inc(pe_passed, 1)
                if jt0 == 0 and it == 4:
                    pe.wait_ge(u_copied, TP - 2)
                for jt in range(jt0, jt1):
                    last = nc.tensor.matmul(bank[SP_BANKS[it % ring]][:, 0:3 * F], adj8[:, jt, it * P:(it + 1) * P].bitcast(FP8),
                                            parts_of[:, w, jt, :, :].rearrange("p q f -> p (q f)"), start=(jt == 0), stop=(jt == T - 1))
                if jt1 == T:
                    last.then_inc(sp_done, 1)

            def spmm_pass(p, w):
                for m, end in enumerate(RHS_ENDS):
                    pe.wait_ge(rhs_ready, len(RHS_ENDS) * p + m + 1)
                    pe.sem_inc(pe_passed, 1)
                    for it in range(len(SP_BANKS)):
                        spmm_part(it, T * p, w, RHS_ENDS[m - 1] if m else 0, end)
                for it in range(len(SP_BANKS), T):
                    spmm_part(it, T * p, w, 0, T)

            pe.wait_ge(w2_loaded, 2 * K * 16)
            def products_u(k):
                if k >= 4:
                    pe.wait_ge(u_copied, k - 3)
                nc.tensor.matmul(bank[k % 4][:, 0:3 * P], xt8[:, k // 4 % 2, k % 4 * P:(k % 4 + 1) * P],
                                 w2_d[:, 1:K, :].rearrange("p m o -> p (m o)"), start=True, stop=True).then_inc(u_done, 1)

            for j in range(GROUPS):
                pe.wait_ge(x2_ready, j + 1)
                transpose_group(feat, bank[6], j).then_inc(xt_done, 1)
                if j >= 1:
                    products_u(4 * j - 4)
                    products_u(4 * j - 3)
                    pe.wait_ge(b3_copied, j)
                pe.wait_ge(xt_copied, j + 1)
                for k in range(4):
                    last = nc.tensor.matmul(bank[7][:, k * P:(k + 1) * P], xt8[:, j % 2, k * P:(k + 1) * P], w2_d[:, 0, :], start=True, stop=True)
                last.then_inc(b3_done, 1)
                if j >= 1:
                    products_u(4 * j - 2)
                    products_u(4 * j - 1)
            for k in range(TP - 4, TP):
                products_u(k)
            pe.wait_ge(b3_copied, GROUPS)

            with pe.Fori(0, K // 2) as i:
                for w in range(2):
                    spmm_pass(2 * i + w, w)

        @block.vector
        def _(dve):
            chain = Chain(dve, dve_did)
            v = nc.vector
            for buf in (w0_d[:, :], w1_d[:, :, :]):
                chain(v.memset(buf, 0.0))
            chain(v.memset(epsc[:, :], EPS))
            chain.wait()
            dve.sem_inc(w_zeroed, 1)
            v.memset(zeros, 0.0).then_inc(zero_ready, 1)

            dve.wait_ge(w_loaded, 16 * 8)
            att_b = g_val[:, 0:4, :, :].rearrange("p t e c -> p (t e c)")
            for m in range(2):
                for e in range(2):
                    rows = slice(e * F, (e + 1) * F)
                    tmp = g_val[rows, 4:6, :, :].rearrange("p t e c -> p (t e c)")[:, 0:F]
                    chain.do(v.tensor_tensor(tmp, w1_d[rows, e, 0:F], att_b[rows, m * F:(m + 1) * F], ALU.mult))
                    chain.do(v.tensor_reduce(w1_d[rows, e, F + m * H:F + (m + 1) * H],
                                             tmp.rearrange("p (h d) -> p h d", d=D), AX_X, ALU.add))
            dve.sem_inc(w1_ready, 1)

            for grp in range(GROUPS):
                dve.wait_ge(prod_done, grp + 1)
                v.tensor_copy(xw[:, 8 * grp:8 * grp + 8, :].rearrange("p a f -> p (a f)"), bank[6 + grp % 2][:, :]).then_inc(prod_copied, 1)
            dve.wait_ge(prod_copied, GROUPS)
            dve.wait_ge(prod_done, GROUPS + 4)

            def split(dst, val, res):
                chain.do(v.tensor_copy(dst[0], val))
                chain.do(v.tensor_tensor(res, val, dst[0], ALU.subtract))
                chain.do(v.tensor_copy(dst[1], res))
                chain.do(v.tensor_tensor(res, res, dst[1], ALU.subtract))
                return v.tensor_copy(dst[2], res)

            def cast_rows(j, r, n, first=False):
                dve.wait_ge(rows_free, j + 1)
                for c in range(2):
                    q = r % 2 * 2 + c
                    dve.wait_ge(stage_loaded[q], 16 * n)
                    v.tensor_scalar(row_buf[r][:, c * NH // 4:(c + 1) * NH // 4].bitcast(U8), stage[q], ONE_FP8, 0.0, ALU.mult, ALU.add,
                                    accum_out=deg2[:, c, bass.ds(j, 1)]).then_inc(stage_read_dve, 1)
                    if c == 0 and not first:
                        inverse_root(j - 1)
                dve.wait_ge(stage_read_dve, 2 * j + 2)
                v.tensor_tensor(deg[:, bass.ds(j, 1)], deg2[:, 0, bass.ds(j, 1)], deg2[:, 1, bass.ds(j, 1)], ALU.add).then_inc(deg_ready, 1)

            def inverse_root(j):
                dve.wait_ge(root_ready, j + 1)
                v.reciprocal(dinv[:, bass.ds(j, 1)], root[:, bass.ds(j, 1)]).then_inc(dinv_ready, 1)

            cast_rows(0, 0, 1, first=True)
            with dve.Fori(0, T // 4 - 1) as i:
                for r in range(1, 5):
                    cast_rows(4 * i + r, r % 4, 2 * i + r // 2 + 1)
            for r in range(1, 4):
                cast_rows(T - 4 + r, r, HALF - 2 + r // 2 + 1)
            inverse_root(T - 1)
            dve.wait_ge(dinv_ready, T)

            norms = [0]

            def layer_norm(dst, val, tmp, t0, t1):
                norms[0] += 1
                st = stat[:, t0:t1]
                chain.do(v.tensor_reduce(st, val, AX_X, ALU.add))
                chain.do(v.scalar_tensor_tensor(val, bcast(st, F), -1.0 / F, val, ALU.mult, ALU.add))
                chain.do(v.tensor_tensor(tmp, val, val, ALU.mult))
                v.tensor_reduce(st, tmp, AX_X, ALU.add).then_inc(var_ready, 1)
                dve.wait_ge(std_ready, norms[0])
                chain.do(v.reciprocal(st, root[:, t0:t1]))
                return v.tensor_tensor(dst, val, bcast(st, F), ALU.mult)

            def centre(val, b):
                val, st = val[:, 8 * b:8 * b + 8, :], stat[:, 8 * b:8 * b + 8]
                chain.do(v.tensor_reduce(st, val, AX_X, ALU.add))
                v.scalar_tensor_tensor(val, bcast(st, F), -1.0 / F, val, ALU.mult, ALU.add).then_inc(centred, 1)

            def square_sums(sq, b, n):
                dve.wait_ge(squared, n)
                v.tensor_reduce(stat[:, 8 * b:8 * b + 8], sq[:, 8 * b:8 * b + 8, :], AX_X, ALU.add).then_inc(var_ready, 1)
                norms[0] += 1

            def scale_rows(dst, val, b, n):
                st = stat[:, 8 * b:8 * b + 8]
                dve.wait_ge(std_ready, n)
                chain.do(v.reciprocal(st, root[:, 8 * b:8 * b + 8]))
                return v.tensor_tensor(dst[:, 8 * b:8 * b + 8, :], val[:, 8 * b:8 * b + 8, :], bcast(st, F), ALU.mult)

            dve.wait_ge(zb_ready, 1)
            for b in range(GROUPS + 2):
                if b < GROUPS:
                    t0, t1 = 8 * b, 8 * b + 8
                    if b == 0:
                        dve.wait_ge(bank_summed, (GROUPS - 1) * (T - 1) + 1)
                        chain.do(v.tensor_tensor(work[:, t0:t1, :], bank[0][:, :].rearrange("p (t f) -> p t f", f=F),
                                                 bcast(dinv[:, t0:t1], F), ALU.mult))
                    else:
                        dve.wait_ge(l0_evacuated, t1 - 8)
                    chain.do(v.tensor_tensor(work[:, t0:t1, :], work[:, t0:t1, :], xw[:, t0:t1, :], ALU.add))
                    chain.do(v.scalar_tensor_tensor(work[:, t0:t1, :], work[:, t0:t1, :], 0.0, feat[:, t0:t1, :], ALU.max, ALU.add))
                    centre(work, b)
                if 1 <= b <= GROUPS:
                    square_sums(xw, b - 1, b)
                if b == GROUPS:
                    scale_rows(x1, work, b - 1, b).then_inc(x1_ready, 1)
                if b >= 2:
                    for m in range(2 * b - 4, 2 * b - 2):
                        dve.wait_ge(feat_done, m + 1)
                        pr4 = bank[6 + m % 2][:, 0:4 * FN].rearrange("p (a n) -> p a n", a=4)
                        chain(v.tensor_copy(feat[:, 4 * m:4 * m + 4, :], pr4[:, :, 0:F]))
                        v.tensor_copy(fac[:, 0:2, 4 * m:4 * m + 4, :], pr4[:, :, F:FN].rearrange("p a (m h) -> p m a h", m=2)).then_inc(feat_copied, 1)
                if 1 <= b < GROUPS:
                    scale_rows(x1, work, b - 1, b).then_inc(x1_ready, 1)
            dve.wait_ge(feat_copied, 2 * GROUPS)
            chain.wait()
            s_f, n_f = fac[:, 0, :, :], fac[:, 1, :, :]
            v.tensor_reduce(nmax[:, 0, :], n_f.rearrange("p t h -> p h t"), AX_X, ALU.max).then_inc(nmax_part, 1)
            chain(v.tensor_scalar(n_cols[:, 0, :, :].rearrange("p h t -> p t h"), n_f, -1.0, None, ALU.mult))
            chain(v.tensor_scalar(n_cols[:, 1, :, :].rearrange("p h t -> p t h"), n_f, STEP, None, ALU.mult))
            dve.wait_ge(nmax_ready, 1)
            top = nmax[:, 1, :].unsqueeze(1).to_broadcast([P, T, H])
            chain.do(v.tensor_tensor(fac[:, 1, :, :], n_f, top, ALU.subtract))
            v.tensor_scalar(fac[:, 3, :, :], fac[:, 1, :, :], SLOPE, None, ALU.mult).then_inc(exp_in, 1)
            dve.wait_ge(srow_done, GROUPS)
            chain.do(v.tensor_tensor(fac[:, 0, :, :], s_f, top, ALU.add))
            chain.do(v.tensor_scalar(fac[:, 2, :, :], fac[:, 0, :, :], 0.0, -(1.0 - SLOPE), ALU.max, ALU.mult))
            v.tensor_scalar(fac[:, 0, :, :], fac[:, 0, :, :], 0.0, 1.0 - SLOPE, ALU.min, ALU.mult).then_inc(exp_in, 1)

            mine_of = [on_dve(k) for k in range(STEPS)]
            nd, na = sum(mine_of), STEPS - sum(mine_of)
            dve.wait_ge(srow_copied, 4)

            def evac_head(pr, e, part):
                for m in (2 * part, 2 * part + 1):
                    t0, t1 = m * PER_BANK, min(T, (m + 1) * PER_BANK)
                    ins = v.tensor_reduce(r_h[:, e, t0:t1, :], bank[SUM_BANKS[e][m]][:, 0:(t1 - t0) * C3].rearrange("p (t q c) -> p t c q", q=3, c=C), AX_X, ALU.add)
                    if m % 2 == 0 or part == 0:
                        chain(ins)
                if part == 1:
                    ins.then_inc(acc_free, 1)

            def evac_sd(pr, m):
                dve.wait_ge(sd_done, HALF * pr + m + 1)
                v.tensor_reduce(s_d[:, 2 * m:2 * m + 2, :, :].rearrange("p t e c -> p (t e) c"),
                                bank[4 + m % 2][:, 0:2 * C3].rearrange("p (t q c) -> p t c q", t=4, q=3), AX_X, ALU.add)\
                    .then_inc(sd_free, 1)

            def conj(pr, k):
                if mine_of[k]:
                    dve.wait_ge(cmp_dve, nd * pr + sum(mine_of[:k + 1]))
                else:
                    dve.wait_ge(cmp_act, na * pr + (k + 1 - sum(mine_of[:k + 1])))
                m32 = mask[k % RING].bitcast(I32)
                a32 = adj8[:, k % T, :].bitcast(I32)
                v.tensor_tensor(m32, m32, a32, ALU.bitwise_and).then_inc(mask_ready, 1)

            first = mine_of.index(True)

            def compare(pr, k):
                e = k // T
                if k % T == mine_of[e * T:].index(True):
                    dve.wait_ge(row_loaded[e], row_of(pr, e))
                dve.wait_ge(mask_free, buffer_free(pr, k))
                v.tensor_scalar(mask[k % RING].bitcast(U8), s_row[e], n_cur[:, k:k + 1], ONE_FP8, ALU.is_gt, ALU.mult)\
                    .then_inc(cmp_dve, 1)

            def finish_tail(pr):
                evac_head(pr, 1, 0)
                chain.wait()
                dve.wait_ge(acc_free, 2 * pr + 3)
                dve.wait_ge(sd_free, HALF * pr + HALF + 2)
                dve.sem_inc(sums_ready, 1)

            def finish_head(pr, e):
                dve.wait_ge(sd_done, HALF * pr + HALF // 2 * (e + 1))
                evac_head(pr, e, 1)

            def begin(pr):
                v.tensor_copy(n_cur, n_cols[:, 0, bass.ds(2 * pr, 2), :].rearrange("p h t -> p (h t)")).then_inc(cols_ready, 1)
                dve.wait_ge(cols_ready, pr + 1)
                compare(pr, first)
                finish_head(pr - 1, 1)
                dve.wait_ge(g_made, pr)
                v.tensor_copy(aux[:, 0:T * C3].bitcast(BF16), aux[:, T * C3:2 * T * C3].bitcast(BF16)).then_inc(g_loaded, 1)

            def steps(pr, k0, k1, done=(first,)):
                for k in range(k0, k1):
                    if k < STEPS and mine_of[k] and k not in done:
                        compare(pr, k)
                    if k >= 1:
                        conj(pr, k - 1)
                    if k == 7:
                        dve.wait_ge(sums_used, pr + 1)
                    if k in (T, STEPS):
                        dve.wait_ge(cmp_dve, nd * pr + sum(mine_of[:k]))
                        dve.sem_inc(row_free[k // T - 1], 1)
                    if k >= 7 and k % 4 == 3:
                        evac_sd(pr, (k - 7) // 4)
                    if k == T + 1:
                        finish_head(pr, 0)
                        evac_head(pr, 0, 0)

            v.tensor_copy(n_cur, n_cols[:, 0, 0:2, :].rearrange("p h t -> p (h t)")).then_inc(cols_ready, 1)
            dve.wait_ge(exp_out, 1)
            prepare(v, chain, 0, g).then_inc(g_loaded, 1)
            dve.wait_ge(cols_ready, 1)
            steps(0, 0, 4, done=())
            with dve.Fori(0, PAIRS - 1) as pr:
                chain.body(pr, 2 * 3)
                steps(pr, 4, STEPS + 1)
                begin(pr + 1)
                steps(pr + 1, 0, 2)
                evac_sd(pr, HALF - 1)
                steps(pr + 1, 2, 4)
                finish_tail(pr)
                chain.end(PAIRS - 1)
            steps(PAIRS - 1, 4, 8)
            v.reciprocal(den[:, :, 0:H - 2], den[:, :, 0:H - 2]).then_inc(den_inverted, 1)
            steps(PAIRS - 1, 8, STEPS + 1)
            finish_head(PAIRS - 1, 1)
            evac_sd(PAIRS - 1, HALF - 1)
            finish_tail(PAIRS - 1)

            dve.wait_ge(exp_out, 2)
            dve.wait_ge(sums_used, PAIRS)
            combine(v, chain, PAIRS - 1)
            chain.do(v.reciprocal(den[:, :, H - 2:H], den[:, :, H - 2:H]))
            chain.do(divide(v, chain, H - 2, H))
            dve.wait_ge(divided, 1)

            dve.wait_ge(x1_back, 16)
            for b in range(GROUPS + 4):
                if b < GROUPS:
                    t0, t1 = 8 * b, 8 * b + 8
                    fg = feat[:, t0:t1, :]
                    chain.do(v.scalar_tensor_tensor(fg, fg, 0.0, x1_b[:, t0:t1, :], ALU.max, ALU.add))
                    centre(feat, b)
                if 1 <= b <= GROUPS:
                    square_sums(scratch, b - 1, GROUPS + b)
                if 3 <= b < GROUPS + 3:
                    t0, t1 = 8 * b - 24, 8 * b - 16
                    dve.wait_ge(part_cast[0], b - 2)
                    v.tensor_tensor(scratch[:, t0:t1, :], b_3[:, t0:t1, :], parts[:, t0:t1, 0, :], ALU.subtract).then_inc(rest_ready, 1)
                if 4 <= b:
                    t0, t1 = 8 * b - 32, 8 * b - 24
                    dve.wait_ge(part_cast[1], b - 3)
                    v.tensor_tensor(scratch[:, t0:t1, :], scratch[:, t0:t1, :], parts[:, t0:t1, 1, :], ALU.subtract).then_inc(rest2_ready, 1)
                if 1 <= b <= GROUPS:
                    scale_rows(feat, feat, b - 1, GROUPS + b).then_inc(x2_ready, 1)

            dve.wait_ge(u_copied, TP)
            chain(v.tensor_tensor(acc[:, 1, :, :], acc[:, 1, :, :], b_3, ALU.subtract))
            chain(v.tensor_tensor(acc[:, 2, :, :], acc[:, 2, :, :], feat[:, :, :], ALU.add))
            chain.wait()
            dve.wait_ge(part_cast[2], GROUPS)
            res = aux[:, 0:4 * F].rearrange("p (a f) -> p a f", f=F)

            def new_pair(p, k, scale, dst):
                for a in range(2):
                    dve.wait_ge(sp_done, T * p + 2 * k + a + 1)
                    v.tensor_reduce(res[:, a, :], bank[SP_BANKS[(2 * k + a) % 6]][:, 0:3 * F].rearrange("p (q f) -> p f q", q=3), AX_X, ALU.add)\
                        .then_inc(sp_free, 1)
                dve.wait_ge(sp_free, T * p + 2 * k + 2 + T % len(SP_BANKS))
                u_p = acc[:, bass.ds(p, 1), 2 * k:2 * k + 2, :].rearrange("p m a f -> p (m a) f")
                chain.do(v.scalar_tensor_tensor(u_p if dst is None else dst, res[:, 0:2, :], scale, u_p, ALU.mult, ALU.add))
                return u_p

            assert K - 2 == 2
            with dve.Fori(0, K - 2) as p:
                chain.body(p, TP * 6)
                chain.passed = dve_passed
                for k in range(TP):
                    b_pair = new_pair(p, k, 2.0, None)
                    dst = parts_of[:, bass.ds(1 - p, 1), 2 * k:2 * k + 2, :, :].rearrange("p w t q f -> p (w t) q f")
                    chain.do(split([dst[:, :, q, :] for q in range(3)], b_pair, res[:, 2:4, :]))
                    if 2 * k + 2 in RHS_ENDS:
                        dve.sem_inc(rhs_ready, 1)
                chain.end(K - 2)
                chain.passed = None
            chain.do(v.tensor_tensor(acc[:, 2, :, :], acc[:, 2, :, :], acc[:, 0, :, :], ALU.subtract))

            def x3_tiles(b, stages):
                t0, t1 = 8 * b, 8 * b + 8
                x3, tmp, st = feat[:, t0:t1, :], scratch[:, 8:16, :], stat[:, t0:t1]
                hi, mid, lo = [parts_of[:, (K - 1) % 2, t0:t1, q, :] for q in range(3)]
                if 0 in stages:
                    chain.do(v.tensor_reduce(st, x3, AX_X, ALU.add))
                    chain.do(v.scalar_tensor_tensor(x3, bcast(st, F), -1.0 / F, x3, ALU.mult, ALU.add))
                if 1 in stages:
                    chain.do(v.tensor_tensor(tmp, x3, x3, ALU.mult))
                    v.tensor_reduce(st, tmp, AX_X, ALU.add).then_inc(var_ready, 1)
                    norms[0] += 1
                if 2 in stages:
                    dve.wait_ge(std_ready, 2 * GROUPS + b + 1)
                    chain.do(v.reciprocal(st, root[:, t0:t1]))
                    chain.do(v.tensor_tensor(x3, x3, bcast(st, F), ALU.mult))
                if 3 in stages:
                    chain.do(v.tensor_copy(hi, x3))
                    chain.do(v.tensor_tensor(tmp, x3, hi, ALU.subtract))
                    chain.do(v.tensor_copy(mid, tmp))
                    chain.do(v.tensor_tensor(tmp, tmp, mid, ALU.subtract))
                    chain.do(v.tensor_copy(lo, tmp))

            for k in range(TP):
                new_pair(K - 2, k, 1.0, feat[:, 2 * k:2 * k + 2, :])
                if k >= 4:
                    x3_tiles((k - 4) // 4, [(k - 4) % 4])
                if k - 3 in (TP // 2, TP - 4):
                    dve.sem_inc(rhs_ready, 1)
            x3_tiles(GROUPS - 1, range(4))
            dve.sem_inc(rhs_ready, 1)

            for t0, t1 in L3_STEPS:
                x3, ax, y = feat[:, t0:t1, :], acc[:, 1, t0:t1, :], acc[:, 0, t0:t1, :]
                chain.do(v.tensor_scalar(y, x3, -0.1, 1.0, ALU.mult, ALU.add))
                chain.do(v.tensor_tensor(y, y, x3, ALU.add))
                for it in range(t0, t1):
                    dve.wait_ge(sp_done, T * (K - 1) + it + 1)
                    v.tensor_reduce(acc[:, 1, it, :], bank[SP_BANKS[it % 6]][:, 0:3 * F].rearrange("p (q f) -> p f q", q=3), AX_X, ALU.add)\
                        .then_inc(sp_free, 1)
                dve.wait_ge(sp_free, T * (K - 1) + t1 + T % len(SP_BANKS))
                chain.do(v.scalar_tensor_tensor(ax, ax, 0.01, x3, ALU.mult, ALU.mult))
                chain.do(v.tensor_reduce(stat[:, t0:t1], ax, AX_X, ALU.add))
                chain.do(v.tensor_tensor(y, y, bcast(stat[:, t0:t1], F), ALU.subtract))
                layer_norm(x3, y, ax, t0, t1).then_inc(out_ready, 1)


_INS = ['x', 'adj', 'L0_gnn_W', 'L0_gnn_b', 'L1_gnn_W', 'L1_gnn_att_self', 'L1_gnn_att_neigh', 'L1_gnn_bias', 'L2_gnn_weight']


def kernel(**inputs):
    import numpy as _np
    import concourse.bacc as _bacc
    from concourse import mybir as _mybir
    from concourse.bass_utils import run_bass_kernel_spmd as _run

    nc = _bacc.Bacc("TRN2", target_bir_lowering=False, num_devices=1, dynamic_dma_scratch_size=1024)
    arrays, args = {}, []
    for name in _INS:
        a = _np.ascontiguousarray(inputs[name])
        arrays[f"in_{name}_dram"] = a
        args.append(nc.dram_tensor(f"in_{name}_dram", a.shape, _mybir.dt.from_np(a.dtype), kind="ExternalInput").ap())
    n, f = inputs["x"].shape
    args.append(nc.dram_tensor("out_0_dram", (n, f), _mybir.dt.float32, kind="ExternalOutput").ap())
    args.append(nc.dram_tensor("scratch_rows", (n // 128 * inputs["L1_gnn_att_self"].shape[0], 128), _mybir.dt.float32, kind="Internal").ap())
    args.append(nc.dram_tensor("scratch_x", (n, f), _mybir.dt.float32, kind="Internal").ap())
    graph_layers(nc, *args)
    r = _run(nc, [arrays], core_ids=[0])
    return r.results[0]["out_0_dram"]
```
